# Optimizing a Trainium2 kernel written in Bass

```python
import numpy as np
import jax
import jax.numpy as jnp

def _softmax(x, axis=-1):
    return jax.nn.softmax(x, axis=axis)

def _gelu(x):
    return jax.nn.gelu(x, approximate=True)

def _silu(x):
    return jax.nn.silu(x)

def _sigmoid(x):
    return jax.nn.sigmoid(x)

def _layernorm(x, axis=-1, eps=1e-05):
    m = jnp.mean(x, axis=axis, keepdims=True)
    v = jnp.var(x, axis=axis, keepdims=True)
    return (x - m) / jnp.sqrt(v + eps)

def _scatter_add(tgt, idx, src, axis=0):
    return tgt.at[idx].add(src)

def _segment_sum(src, seg, n):
    return jax.ops.segment_sum(src, seg, n)
kernel_name = 'mk_sandwich_d1_jaxref_r4_e4b3e1'

def setup_inputs(seed: int=0):
    np.random.seed(seed)
    _w = jnp.asarray

    def _L0_attn_setup():
        import jax, jax.numpy as jnp
        import numpy as np
        LN_EPS = 1e-05
        U_T = 1.0
        key = jax.random.key(seed)
        B, L, D, H = (2, 512, 256, 16)
        dk = D // H
        ks = jax.random.split(key, 4)
        x = jax.random.normal(ks[0], (B, L, D), jnp.float32)
        W_qkv = jax.random.normal(ks[1], (3 * D, D), jnp.float32) / np.sqrt(D)
        W_o = jax.random.normal(ks[2], (D, D), jnp.float32) / np.sqrt(D)
        W_LTM = jax.random.normal(ks[3], (H, dk, dk), jnp.float32) * 0.5
        return {'x': x, 'W_qkv': W_qkv, 'W_o': W_o, 'W_LTM': W_LTM, 'V_gs': jnp.zeros((H,), jnp.float32), 'V_T0': jnp.zeros((H,), jnp.float32), 'beta_tau': jnp.ones((H,), jnp.float32), 'beta_gm': jnp.ones((H,), jnp.float32) * 0.1, 'C_ch': jnp.ones((H,), jnp.float32), 'gamma': jnp.ones((H,), jnp.float32) * 0.1, 'alpha_ppd': jnp.ones((1,), jnp.float32), 'IC_threshold': jnp.ones((1,), jnp.float32)}
    _L0_attn_in = _L0_attn_setup()

    def _L0_ffn_setup():
        import jax, jax.numpy as jnp
        import numpy as np
        import math
        BETA = 0.9
        THRESHOLD = 1.0
        NUM_STEPS = 5
        ALPHA = 2.0

        @jax.custom_vjp
        def spike_fn(u):
            return (u > 0).astype(u.dtype)

        def _spike_fwd(u):
            return (spike_fn(u), u)

        def _spike_bwd(u, g):
            s = jnp.pi / 2.0 * ALPHA * u
            return (g * (ALPHA / 2.0) / (1.0 + s * s),)
        spike_fn.defvjp(_spike_fwd, _spike_bwd)
        key = jax.random.key(seed)
        k1, k2, k3 = jax.random.split(key, 3)
        n_embd = 256
        x = jax.random.normal(k1, (4, 512, n_embd), dtype=jnp.float32)
        W_fc = jax.random.normal(k2, (4 * n_embd, n_embd), dtype=jnp.float32) / math.sqrt(n_embd)
        W_proj = jax.random.normal(k3, (n_embd, 4 * n_embd), dtype=jnp.float32) / math.sqrt(4 * n_embd)
        return {'x': x, 'W_fc': W_fc, 'W_proj': W_proj}
    _L0_ffn_in = _L0_ffn_setup()
    _d = {'L0_attn_x': _L0_attn_in['x'], 'L0_attn_W_qkv': _L0_attn_in['W_qkv'], 'L0_attn_W_o': _L0_attn_in['W_o'], 'L0_attn_W_LTM': _L0_attn_in['W_LTM'], 'L0_attn_V_gs': _L0_attn_in['V_gs'], 'L0_attn_V_T0': _L0_attn_in['V_T0'], 'L0_attn_beta_tau': _L0_attn_in['beta_tau'], 'L0_attn_beta_gm': _L0_attn_in['beta_gm'], 'L0_attn_C_ch': _L0_attn_in['C_ch'], 'L0_attn_gamma': _L0_attn_in['gamma'], 'L0_attn_alpha_ppd': _L0_attn_in['alpha_ppd'], 'L0_attn_IC_threshold': _L0_attn_in['IC_threshold'], 'L0_ffn_W_fc': _L0_ffn_in['W_fc'], 'L0_ffn_W_proj': _L0_ffn_in['W_proj']}
    _x0 = _d['L0_attn_x']
    _d['L0_attn_x'] = jax.random.normal(jax.random.fold_in(jax.random.key(seed), 1), (8, 512, 256), dtype=_x0.dtype)
    del _x0
    return _d

def reference(L0_attn_x, L0_attn_W_qkv, L0_attn_W_o, L0_attn_W_LTM, L0_attn_V_gs, L0_attn_V_T0, L0_attn_beta_tau, L0_attn_beta_gm, L0_attn_C_ch, L0_attn_gamma, L0_attn_alpha_ppd, L0_attn_IC_threshold, L0_ffn_W_fc, L0_ffn_W_proj):

    def _L0_attn_ref(x, W_qkv, W_o, W_LTM, V_gs, V_T0, beta_tau, beta_gm, C_ch, gamma, alpha_ppd, IC_threshold):
        import jax, jax.numpy as jnp
        import numpy as np
        LN_EPS = 1e-05
        U_T = 1.0
        B, L, D = x.shape
        H, dk, _ = W_LTM.shape
        qkv = (x @ W_qkv.T).reshape(B, L, 3, H, dk)
        q, k, v = (qkv[:, :, 0], qkv[:, :, 1], qkv[:, :, 2])
        mu = k.mean(-1, keepdims=True)
        var = ((k - mu) ** 2).mean(-1, keepdims=True)
        k = (k - mu) / jnp.sqrt(var + LN_EPS)
        V_norm = (V_gs[:, None, None] - V_T0[:, None, None] + W_LTM) / U_T
        sp = jax.nn.softplus(V_norm)
        g_ch = beta_tau[:, None, None] * sp
        retention = jnp.exp(-g_ch / C_ch[:, None, None])
        G = beta_gm[:, None, None] * sp * jax.nn.sigmoid(V_norm)
        sign_mask = jnp.tanh(alpha_ppd * (g_ch - IC_threshold))
        coef = gamma[:, None, None] * sign_mask * G
        qL = jnp.moveaxis(q, 1, 0)
        kL = jnp.moveaxis(k, 1, 0)
        vL = jnp.moveaxis(v, 1, 0)

        def step(F, qkv_t):
            q_t, k_t, v_t = qkv_t
            hebbian = jnp.einsum('bhd,bhe->bhde', v_t, k_t)
            F = retention * F + coef * hebbian
            y_t = jnp.einsum('bhde,bhe->bhd', W_LTM + F, q_t)
            return (F, y_t)
        F0 = jnp.zeros((B, H, dk, dk), x.dtype)
        _, yL = jax.lax.scan(step, F0, (qL, kL, vL))
        y = jnp.moveaxis(yL, 0, 1).reshape(B, L, D)
        return y @ W_o.T

    def _L0_ffn_ref(x, W_fc, W_proj):
        import jax, jax.numpy as jnp
        import numpy as np
        import math
        BETA = 0.9
        THRESHOLD = 1.0
        NUM_STEPS = 5
        ALPHA = 2.0

        @jax.custom_vjp
        def spike_fn(u):
            return (u > 0).astype(u.dtype)

        def _spike_fwd(u):
            return (spike_fn(u), u)

        def _spike_bwd(u, g):
            s = jnp.pi / 2.0 * ALPHA * u
            return (g * (ALPHA / 2.0) / (1.0 + s * s),)
        spike_fn.defvjp(_spike_fwd, _spike_bwd)
        h = jnp.square(jax.nn.relu(jnp.einsum('bsd,fd->bsf', x, W_fc)))
        y = jnp.einsum('bsf,df->bsd', h, W_proj)

        def step(mem, _):
            reset = jax.lax.stop_gradient(spike_fn(mem - THRESHOLD))
            mem_new = BETA * mem + y - reset * THRESHOLD
            spk = spike_fn(mem_new - THRESHOLD)
            return (mem_new, spk)
        mem0 = jnp.zeros_like(y)
        _, spks = jax.lax.scan(step, mem0, None, length=NUM_STEPS)
        return jnp.sum(spks, axis=0) / NUM_STEPS
    x = L0_attn_x
    x = x + _layernorm(_L0_attn_ref(_layernorm(x, axis=-1), L0_attn_W_qkv, L0_attn_W_o, L0_attn_W_LTM, L0_attn_V_gs, L0_attn_V_T0, L0_attn_beta_tau, L0_attn_beta_gm, L0_attn_C_ch, L0_attn_gamma, L0_attn_alpha_ppd, L0_attn_IC_threshold), axis=-1)
    x = x + _layernorm(_L0_ffn_ref(_layernorm(x, axis=-1), L0_ffn_W_fc, L0_ffn_W_proj), axis=-1)
    return x

_drawn_inputs = setup_inputs


def setup_inputs(seed=0):
    import zlib

    import numpy as np

    out = dict(_drawn_inputs(seed))
    spreads = {'L0_attn_V_gs': (0.0, 2.0),
     'L0_attn_V_T0': (0.0, 2.0),
     'L0_attn_beta_tau': (1.0, 0.6),
     'L0_attn_beta_gm': (0.10000000149011612, 0.6),
     'L0_attn_C_ch': (1.0, 0.6),
     'L0_attn_gamma': (0.10000000149011612, 0.6)}
    factors = {}
    for name, (base, spread) in spreads.items():
        noise = np.random.default_rng([zlib.crc32(name.encode()), seed]).standard_normal(out[name].shape)
        drawn = base * np.exp(spread * noise) if base else spread * noise
        out[name] = jnp.asarray(drawn.astype(out[name].dtype))
    for name, factor in factors.items():
        out[name] = (out[name] * factor).astype(out[name].dtype)
    return out
```

```python
from contextlib import ExitStack

import numpy as np

import concourse.bass as bass
from concourse import mybir

F32 = mybir.dt.float32
ALU = mybir.AluOpType
ACT = mybir.ActivationFunctionType
AX = mybir.AxisListType

B, L, D, H, DK, F = 8, 512, 256, 16, 16, 1024
P = 128
KT = D // P
HALVES = KT
HH = H // HALVES
C = L // 2
TILES = L // P
FT = F // P
GRP = 4
SLOTS = 16
HS = SLOTS // HALVES
NS = 4
NZ = 8
LN_EPS = 1e-5
STEPS, BETA, THRESHOLD = 5, 0.9, 1.0


def spike_count(y):
    mem, spikes = np.float32(0), 0
    for _ in range(STEPS):
        reset = np.float32(mem - np.float32(THRESHOLD) > 0)
        mem = np.float32(np.float32(BETA) * mem + y) - reset * np.float32(THRESHOLD)
        spikes += int(mem - np.float32(THRESHOLD) > 0)
    return spikes


def spike_drives():
    out = []
    for k in range(1, STEPS + 1):
        low, high = np.float32(0), np.float32(2)
        while np.nextafter(low, high, dtype=np.float32) < high:
            mid = np.float32((low + high) / 2)
            low, high = (mid, high) if spike_count(mid) < k else (low, mid)
        out.append(float(low))
    return out


DRIVES = spike_drives()


def step_features(s):
    j = s % HS
    first = j // 2 + 8 * (j % 2)
    return s // HS, (first, first + 4)


def build(nc, x, w_qkv, w_o, w_fc, w_proj, w_ltm, head_params, shared_params, ident, head_mask, pick, out):
    ctx = ExitStack()
    with ctx:
        def sb(name, shape, dt=F32):
            return ctx.enter_context(nc.sbuf_tensor(name, shape, dt))

        def ps(name, shape):
            return ctx.enter_context(nc.psum_tensor(name, shape, F32))

        def sem(name):
            return ctx.enter_context(nc.semaphore(name))

        wqkv_sb = sb("wqkv_sb", [P, KT, 3 * D])
        wo_sb = sb("wo_sb", [P, HALVES, D])
        wfc_sb = sb("wfc_sb", [P, KT, F])
        wproj_sb = sb("wproj_sb", [P, FT, D])
        pick_sb = sb("pick_sb", [P, DK, P])
        ident_sb = sb("ident_sb", [P, P])
        mask_sb = sb("mask_sb", [P, HH])
        mean_sb = sb("mean_sb", [P, HH])
        wt = sb("wt", [P, HALVES * DK])
        hp = sb("hp", [P, 6, HALVES])
        shp = sb("shp", [P, 2])
        vn = sb("vn", [P, HALVES * DK])
        absv, zt, goc, marg, signm, sp_v, t0, t1, t2 = (
            sb(name, [P, HALVES * DK]) for name in "absv zt goc marg signm sp_v t0 t1 t2".split())
        gvt = sb("gvt", [P, HALVES])
        rch = sb("rch", [P, HALVES])
        ret = sb("ret", [P, HALVES * DK])
        ret2 = sb("ret2", [P, HALVES * DK])
        coef = sb("coef", [P, HALVES * DK])
        coefr = sb("coefr", [P, HALVES * DK])
        wblk = sb("wblk", [P, HALVES, DK, HH])
        cblk = sb("cblk", [P, HALVES, DK, HH])
        summer = sb("summer", [P, 2, HALVES, 4, GRP, 4 * HH])
        eps_sb = sb("eps_sb", [P, 2])
        ksum = sb("ksum", [P, KT, H])

        stats = [sb(f"stats{i}", [P, TILES, 6]) for i in range(4)]
        moments = [sb(f"moments{i}", [P, 3, TILES]) for i in range(4)]
        dev = [sb(f"dev{i}", [P, TILES]) for i in range(4)]
        rdev = [sb(f"rdev{i}", [P, TILES]) for i in range(4)]
        nmr = [sb(f"nmr{i}", [P, TILES]) for i in range(4)]

        xa = sb("xa", [P, TILES, D])
        xr = sb("xr", [P, TILES, D])
        xn = sb("xn", [P, TILES, D])
        xt = sb("xt", [P, KT, L])
        kc = sb("kc", [P, L])
        ksq = sb("ksq", [P, L])
        kdev = sb("kdev", [P, TILES * HH])
        krd = sb("krd", [P, TILES * HH])
        krx = sb("krx", [P, TILES * HH, DK])
        kf = sb("kf", [P, HALVES, L])
        qf = sb("qf", [P, HALVES, L])
        vf = sb("vf", [P, HALVES, L])
        qk = sb("qk", [P, HALVES, C])
        dv = sb("dv", [P, HALVES, C])
        hebb = sb("hebb", [P, 2, 2, L])
        pair = sb("pair", [P, 2, 2, C])
        state = sb("state", [P, NS, 2, C + 1])
        prod = sb("prod", [P, NZ, 2, L])
        yt = sb("yt", [P, HALVES, L])
        oo = sb("oo", [P, TILES, D])
        on = sb("on", [P, TILES, D])
        x1 = sb("x1", [P, TILES, D])
        x1k = sb("x1k", [P, TILES, D])
        x1n = sb("x1n", [P, TILES, D])
        x1t = sb("x1t", [P, KT, L])
        hr = sb("hr", [P, 2, L])
        ht = sb("ht", [P, FT, L])
        yf = sb("yf", [P, TILES, D])
        spk = sb("spk", [P, TILES, D])
        sn = sb("sn", [P, TILES, D])
        res = sb("res", [P, TILES, D])

        p_rep = [ps(f"p_rep{i}", [P, 2, L]) for i in range(2)]
        p_y = [ps(f"p_y{i}", [P, L]) for i in range(HALVES)]
        p_a = ps("p_a", [P, L])
        p_c = ps("p_c", [P, L])

        S = {name: sem(name) for name in """
            x_in params_in tables_in weights_in again_in out_done keep_done
            setup_ready setup_exp centred tables_done setup_step
            n1_stats n1_diff n1_var n1_dev n1_step n1_done  xt_turned xt_done
            k_proj k_sq k_var k_dev k_rdev k_spread k_scale k_done  v_proj v_done  q_proj q_done
            qk_done own_sum dv_done
            rep_done hebb_done pair_done state_done prod_done sum_done y_copied y_done
            o_proj o_done n2_stats n2_diff n2_var n2_dev n2_step n2_done x1_done
            n3_stats n3_diff n3_var n3_dev n3_step n3_done  x1_turned x1t_done
            up_done relu_done h_done down_done yf_done
            spike_step n4_stats n4_diff n4_var n4_dev n4_step n4_done res_done""".split()}

        def at(value):
            return max(value, 0) if isinstance(value, int) else value

        def run(eng, iteration):
            iteration(0, True, False, False, True)
            iteration(1, True, True, False, True)
            with eng.Fori(2, B - 1) as g:
                iteration(g, True, True, True, True)
            iteration(B - 1, True, True, True, False)
            iteration(B, False, True, True, False)
            iteration(B + 1, False, False, True, False)

        def cols(u):
            at = (u % 2) * C + (u // 2) * P
            return slice(at, at + P)

        def x_tiles(a, b):
            return a[bass.ds(b * L, L), :].rearrange("(c p i) d -> p c i d", c=2, i=2)

        def tiles(t):
            return t[:, :, :].rearrange("p (c i) d -> p c i d", c=2)

        block = ctx.enter_context(nc.Block())

        @block.sync
        def _(sp):
            sp.dma_start(tiles(xa), x_tiles(x, 0)).then_inc(S["x_in"], 16)
            sp.dma_start(ident_sb[:, :], ident).then_inc(S["tables_in"], 16)
            sp.dma_start(wqkv_sb[:, :, :], w_qkv.rearrange("(t p) n -> p t n", p=P)).then_inc(S["tables_in"], 16)
            sp.dma_start(mask_sb[:, :], head_mask).then_inc(S["tables_in"], 16)
            sp.dma_start(wt[:, :], w_ltm).then_inc(S["params_in"], 16)
            sp.dma_start(hp[:, :, :], head_params).then_inc(S["params_in"], 16)
            sp.dma_start(shp[:, :], shared_params).then_inc(S["params_in"], 16)
            sp.dma_start(pick_sb[:, :, :], pick).then_inc(S["weights_in"], 16)
            sp.dma_start(wo_sb[:, :, :], w_o.rearrange("(t p) n -> p t n", p=P)).then_inc(S["weights_in"], 16)
            sp.dma_start(wfc_sb[:, :, :], w_fc.rearrange("(t p) n -> p t n", p=P)).then_inc(S["weights_in"], 16)
            sp.dma_start(wproj_sb[:, :, :], w_proj.rearrange("(t p) n -> p t n", p=P)).then_inc(S["weights_in"], 16)

            def iteration(g, now, before, two_before, after):
                if after:
                    sp.wait_ge(S["n1_done"], at(TILES * (g + 1)))
                    sp.dma_start(tiles(xa), x_tiles(x, g + 1)).then_inc(S["x_in"], 16)
                if before:
                    sp.wait_ge(S["x1_done"], at(g - 1))
                    sp.dma_start(tiles(xr), x_tiles(x, g - 1)).then_inc(S["again_in"], 16)
                if two_before:
                    sp.wait_ge(S["res_done"], at(g - 1))
                    sp.dma_start(x_tiles(out, g - 2), tiles(res)).then_inc(S["out_done"], 16)
                if before:
                    sp.wait_ge(S["x1_done"], at(g))
                    sp.dma_start(x1k[:, :, :], x1[:, :, :]).then_inc(S["keep_done"], 16)

            run(sp, iteration)
            sp.wait_ge(S["out_done"], at(16 * B))

        @block.tensor
        def _(pe):
            def turn_x(b, t):
                pe.wait_ge(S["dv_done"], at(2 * b - 1))
                pe.wait_ge(S["xt_done"], at(KT * b + t))
                pe.wait_ge(S["n1_done"], at(TILES * (b + 1)))
                for u in range(TILES):
                    last = pe.matmul(p_a[:, cols(u)], xn[:, u, t * P:(t + 1) * P], ident_sb[:, :],
                                     start=True, stop=True)
                last.then_inc(S["xt_turned"], 1)

            def project(b, first_col, done):
                for t in range(KT):
                    last = pe.matmul(p_a[:, :], wqkv_sb[:, t, first_col:first_col + P], xt[:, t, :],
                                     start=(t == 0), stop=(t == KT - 1))
                last.then_inc(S[done], 1)

            def project_k(b, half):
                pe.wait_ge(S["xt_done"], at(KT * (b + 1)))
                pe.wait_ge(S["k_done"], at(2 * b + half))
                project(b, D + half * P, "k_proj")

            def project_v(b, half):
                pe.wait_ge(S["k_dev"], at(2 * b + half + 1))
                pe.wait_ge(S["dv_done"], at(2 * b))
                project(b, 2 * D + half * P, "v_proj")

            def project_q(b, half):
                pe.wait_ge(S["v_done"], at(2 * b + half + 1))
                project(b, half * P, "q_proj")

            def key_variance(b, half):
                pe.wait_ge(S["k_sq"], at(2 * b + half + 1))
                for u in range(TILES):
                    last = pe.matmul(p_a[:, u * HH:(u + 1) * HH], ksq[:, u * P:(u + 1) * P], mean_sb[:, :],
                                     start=True, stop=True)
                last.then_inc(S["k_var"], 1)

            def key_scale(b, half):
                pe.wait_ge(S["k_spread"], at(2 * b + half + 1))
                pe.wait_ge(S["q_done"], at(2 * b + half + 1))
                for u in range(TILES):
                    scale = krx[:, u * HH:(u + 1) * HH, :].rearrange("p h e -> p (h e)")
                    last = pe.matmul(p_a[:, u * P:(u + 1) * P], scale, ident_sb[:, :], start=True, stop=True)
                last.then_inc(S["k_scale"], 1)

            def own_update(b, half, after):
                pe.wait_ge(S["qk_done"], at(2 * b + half + 1))
                if half == 0:
                    pe.wait_ge(S["k_done"], at(2 * b + 2))
                else:
                    pe.wait_ge(S["dv_done"], at(2 * b + 1))
                    if after:
                        pe.wait_ge(S["k_dev"], at(2 * b + 3))
                pe.matmul(p_a[:, 0:C], cblk[:, half, :, :].rearrange("p d h -> p (d h)"), qk[:, half, :],
                          start=True, stop=True).then_inc(S["own_sum"], 1)

            def replicate(b, s):
                half, features = step_features(s)
                pe.wait_ge(S["hebb_done"], at(SLOTS * b + s - 1))
                if s % HS == 0:
                    pe.wait_ge(S["v_done"], at(2 * b + half + 1))
                for i, d in enumerate(features):
                    last = pe.matmul(p_rep[s % 2][:, i, :], pick_sb[:, d, :], vf[:, half, :], start=True, stop=True)
                last.then_inc(S["rep_done"], 1)

            def sums(b, m):
                half, dl = m // 4, m % 4
                if dl == 0:
                    pe.wait_ge(S["y_copied"], at(2 * (b - 1) + half + 1))
                    pe.wait_ge(S["q_done"], at(2 * b + half + 1))
                    pe.matmul(p_y[half][:, :], wblk[:, half, :, :].rearrange("p d h -> p (d h)"), qf[:, half, :],
                              start=True, stop=False, skip_group_check=True)
                pe.wait_ge(S["prod_done"], at(SLOTS * b + 2 * m + 2))
                for i in range(2):
                    for grp in range(GRP):
                        s = 2 * m + grp // 2
                        last = pe.matmul(p_y[half][32 * grp:32 * grp + 32, i * C:(i + 1) * C],
                                         summer[:, i, half, dl, grp, :], prod[:, s % NZ, grp % 2, i * C:(i + 1) * C],
                                         start=False, stop=(dl == 3), skip_group_check=True)
                last.then_inc(S["sum_done"], 1)

            def project_out(b, t):
                pe.wait_ge(S["relu_done"], at(FT * b))
                pe.wait_ge(S["o_done"], at(2 * b + t))
                pe.wait_ge(S["y_done"], at(2 * (b + 1)))
                for i in range(2):
                    for half in range(HALVES):
                        last = pe.matmul(p_c[:, i * D:(i + 1) * D], yt[:, half, cols(2 * t + i)], wo_sb[:, half, :],
                                         start=(half == 0), stop=(half == HALVES - 1))
                last.then_inc(S["o_proj"], 1)

            def turn_x1(b, t):
                pe.wait_ge(S["o_done"], at(2 * (b + 1)))
                pe.wait_ge(S["yf_done"], at(TILES * b))
                pe.wait_ge(S["x1t_done"], at(KT * b + t))
                pe.wait_ge(S["n3_done"], at(TILES * (b + 1)))
                for u in range(TILES):
                    last = pe.matmul(p_c[:, u * P:(u + 1) * P], x1n[:, u, t * P:(t + 1) * P], ident_sb[:, :],
                                     start=True, stop=True)
                last.then_inc(S["x1_turned"], 1)

            def up(b, f):
                pe.wait_ge(S["x1t_done"], at(KT * (b + 1)))
                pe.wait_ge(S["relu_done"], at(FT * b + f))
                for t in range(KT):
                    last = pe.matmul(p_c[:, :], wfc_sb[:, t, f * P:(f + 1) * P], x1t[:, t, :],
                                     start=(t == 0), stop=(t == KT - 1))
                last.then_inc(S["up_done"], 1)

            def down(b, u, next_too):
                pe.wait_ge(S["h_done"], at(FT * (b + 1)))
                if next_too:
                    pe.wait_ge(S["o_done"], at(2 * (b + 2)))
                pe.wait_ge(S["yf_done"], at(TILES * b + u))
                for f in range(FT):
                    last = pe.matmul(p_c[:, 0:D], ht[:, f, u * P:(u + 1) * P], wproj_sb[:, f, :],
                                     start=(f == 0), stop=(f == FT - 1))
                last.then_inc(S["down_done"], 1)

            pe.wait_ge(S["tables_in"], 48)
            turn_x(0, 0)
            turn_x(0, 1)
            pe.wait_ge(S["centred"], 2)
            project_k(0, 0)
            key_variance(0, 0)
            project_v(0, 0)
            project_q(0, 0)
            key_scale(0, 0)
            pe.wait_ge(S["weights_in"], 64)
            replicate(0, 0)
            pe.wait_ge(S["tables_done"], 1)

            def iteration(g, now, before, two_before, after):
                for s in range(SLOTS):
                    if now and s < SLOTS - 1:
                        replicate(g, s + 1)
                    if now:
                        if s == 0: project_k(g, 1)
                        if s == 1: key_variance(g, 1)
                        if s == 2: project_v(g, 1)
                        if s == 3: project_q(g, 1)
                        if s == 4: key_scale(g, 1)
                        if s == 5: own_update(g, 0, after)
                    if two_before and s < 5:
                        up(g - 2, 3 + s)
                    if before and s == 6:
                        project_out(g - 1, 0)
                        project_out(g - 1, 1)
                    if after:
                        if s == 7: turn_x(g + 1, 0)
                        if s == 7: turn_x(g + 1, 1)
                        if s == 8: project_k(g + 1, 0)
                        if s == 9: key_variance(g + 1, 0)
                    if now and s == 9:
                        own_update(g, 1, after)
                    if after:
                        if s == 10: project_v(g + 1, 0)
                        if s == 11: project_q(g + 1, 0)
                        if s == 13: key_scale(g + 1, 0)
                    if two_before and 7 <= s < 7 + TILES:
                        down(g - 2, s - 7, before)
                    if before and s == 12:
                        turn_x1(g - 1, 0)
                        turn_x1(g - 1, 1)
                    if before and s >= 13:
                        up(g - 1, s - 13)
                    if before and s in (1, 3):
                        sums(g - 1, 6 + s // 2)
                    if now and s >= 5 and s % 2:
                        sums(g, (s - 5) // 2)
                    if after and s == SLOTS - 1:
                        replicate(g + 1, 0)

            run(pe, iteration)

        @block.scalar
        def _(act):
            act.wait_ge(S["setup_ready"], 1)
            nc.scalar.activation(zt[:, :], absv[:, :], ACT.Exp, scale=-1.0).then_inc(S["setup_exp"], 1)
            act.wait_ge(S["setup_ready"], 2)
            nc.scalar.activation(ret[:, :], goc[:, :], ACT.Exp, scale=-1.0)
            nc.scalar.activation(signm[:, :], marg[:, :], ACT.Tanh).then_inc(S["setup_exp"], 1)

            def deviation(n, b):
                act.wait_ge(S[f"n{n}_var"], at(b + 1))
                eps = eps_sb[:, 1:2] if n == 4 else eps_sb[:, 0:1]
                nc.scalar.activation(dev[n - 1][:, :], moments[n - 1][:, 2, :], ACT.Sqrt, bias=eps,
                                     scale=1.0 / D).then_inc(S[f"n{n}_dev"], 1)

            def norm(n, b, src, dst, used, count):
                act.wait_ge(S[f"n{n}_step"], at(2 * (b + 1)))
                act.wait_ge(S[used], at(count))
                for u in range(TILES):
                    nc.scalar.activation(dst[:, u, :], src[:, u, :], ACT.Identity, scale=rdev[n - 1][:, u:u + 1],
                                         bias=nmr[n - 1][:, u:u + 1]).then_inc(S[f"n{n}_done"], 1)

            def copy(src, dst, ready, count, done):
                act.wait_ge(S[ready], at(count))
                nc.scalar.copy(dst, src).then_inc(S[done], 1)

            def norm1(b):
                norm(1, b, xa, xn, "xt_turned", KT * b)

            def copy_xt(b):
                for t in range(KT):
                    copy(p_a[:, :], xt[:, t, :], "xt_turned", KT * b + t + 1, "xt_done")

            def square_k(b, half):
                act.wait_ge(S["k_proj"], at(2 * b + half + 1))
                act.wait_ge(S["k_done"], at(2 * b + half))
                nc.scalar.copy(kc[:, :], p_a[:, :])
                nc.scalar.activation(ksq[:, :], p_a[:, :], ACT.Square).then_inc(S["k_sq"], 1)

            def key_deviation(b, half):
                act.wait_ge(S["k_var"], at(2 * b + half + 1))
                nc.scalar.activation(kdev[:, :], p_a[:, 0:TILES * HH], ACT.Sqrt, bias=eps_sb[:, 0:1]).then_inc(
                    S["k_dev"], 1)

            def copy_v(b, half):
                copy(p_a[:, :], vf[:, half, :], "v_proj", 2 * b + half + 1, "v_done")

            def copy_q(b, half):
                act.wait_ge(S["prod_done"], at(SLOTS * (b - 1) + HS * (half + 1)))
                copy(p_a[:, :], qf[:, half, :], "q_proj", 2 * b + half + 1, "q_done")

            def copy_y(b, half):
                act.wait_ge(S["o_proj"], at(2 * b))
                copy(p_y[half][:, :], yt[:, half, :], "sum_done", HS * b + 4 * (half + 1), "y_copied")

            def copy_o(b, t):
                act.wait_ge(S["n2_done"], at(TILES * b))
                copy(p_c[:, :], oo[:, 2 * t:2 * t + 2, :].rearrange("p u d -> p (u d)"), "o_proj", 2 * b + t + 1,
                     "o_done")

            def copy_x1t(b):
                for t in range(KT):
                    copy(p_c[:, :], x1t[:, t, :], "x1_turned", KT * b + t + 1, "x1t_done")

            def hidden(b, f):
                act.wait_ge(S["up_done"], at(FT * b + f + 1))
                act.wait_ge(S["h_done"], at(FT * b + f - 1))
                nc.scalar.activation(hr[:, f % 2, :], p_c[:, :], ACT.Relu).then_inc(S["relu_done"], 1)
                act.wait_ge(S["relu_done"], at(FT * b + f + 1))
                nc.scalar.activation(ht[:, f, :], hr[:, f % 2, :], ACT.Square).then_inc(S["h_done"], 1)

            def copy_yf(b, u):
                act.wait_ge(S["spike_step"], at(STEPS * b))
                copy(p_c[:, 0:D], yf[:, u, :], "down_done", TILES * b + u + 1, "yf_done")

            deviation(1, 0)
            norm1(0)
            copy_xt(0)
            square_k(0, 0)
            key_deviation(0, 0)
            copy_v(0, 0)
            copy_q(0, 0)

            def iteration(g, now, before, two_before, after):
                b, b1, b2 = g + 1, g - 1, g - 2
                for s in range(SLOTS):
                    if now:
                        if s == 0: square_k(g, 1)
                        if s == 1: key_deviation(g, 1)
                        if s == 2: copy_v(g, 1)
                        if s == 3: copy_q(g, 1)
                    if before and s == 4: copy_y(b1, 1)
                    if two_before and s < 5: hidden(b2, 3 + s)
                    if after and s == 4: deviation(1, b)
                    if after and s == 5: norm1(b)
                    if before and s == 6:
                        copy_o(b1, 0)
                        copy_o(b1, 1)
                    if after and s == 7: copy_xt(b)
                    if before and s == 8:
                        deviation(2, b1)
                        norm(2, b1, oo, on, "x1_done", b1)
                    if after and s == 8: square_k(b, 0)
                    if after and s == 9: key_deviation(b, 0)
                    if two_before and 7 <= s < 7 + TILES: copy_yf(b2, s - 7)
                    if after and s == 10: copy_v(b, 0)
                    if before and s == 11:
                        deviation(3, b1)
                        norm(3, b1, x1, x1n, "x1_turned", KT * b1)
                    if after and s == 11: copy_q(b, 0)
                    if now and s == 12: copy_y(g, 0)
                    if before and s == 12: copy_x1t(b1)
                    if two_before and s == 13:
                        deviation(4, b2)
                        norm(4, b2, spk, sn, "res_done", b2)
                    if before and s >= 13: hidden(b1, s - 13)

            run(act, iteration)

        @block.vector
        def _(dve):
            v = nc.vector
            steps = [0]

            def step(ins):
                steps[0] += 1
                ins.then_inc(S["setup_step"], 1)
                dve.wait_ge(S["setup_step"], steps[0])

            def statistics(n, b, src, ready, count):
                dve.wait_ge(S[ready], at(count))
                dve.wait_ge(S[f"n{n}_var"], at(b))
                for u in range(TILES):
                    last = v.bn_stats(stats[n - 1][:, u, :], src[:, u, :])
                last.then_inc(S[f"n{n}_stats"], 1)
                dve.wait_ge(S[f"n{n}_stats"], at(b + 1))
                dve.wait_ge(S[f"n{n}_step"], at(2 * b))
                st, mo = stats[n - 1], moments[n - 1]
                v.tensor_tensor(mo[:, 0, :], st[:, :, 1], st[:, :, 4], ALU.add)
                v.tensor_tensor(mo[:, 1, :], st[:, :, 1], st[:, :, 4], ALU.subtract).then_inc(S[f"n{n}_diff"], 1)
                v.tensor_tensor(mo[:, 2, :], st[:, :, 2], st[:, :, 5], ALU.add).then_inc(S[f"n{n}_diff"], 1)
                dve.wait_ge(S[f"n{n}_diff"], at(3 * b + 1))
                v.scalar_tensor_tensor(mo[:, 1, :], mo[:, 1, :], D / 4, mo[:, 1, :], ALU.mult, ALU.mult).then_inc(
                    S[f"n{n}_diff"], 1)
                dve.wait_ge(S[f"n{n}_diff"], at(3 * (b + 1)))
                v.tensor_tensor(mo[:, 2, :], mo[:, 2, :], mo[:, 1, :], ALU.add).then_inc(S[f"n{n}_var"], 1)

            def scales(n, b):
                dve.wait_ge(S[f"n{n}_dev"], at(b + 1))
                dve.wait_ge(S[f"n{n}_done"], at(TILES * b))
                v.reciprocal(rdev[n - 1][:, :], dev[n - 1][:, :]).then_inc(S[f"n{n}_step"], 1)
                dve.wait_ge(S[f"n{n}_step"], at(2 * b + 1))
                v.scalar_tensor_tensor(nmr[n - 1][:, :], moments[n - 1][:, 0, :], -0.5, rdev[n - 1][:, :], ALU.mult,
                                       ALU.mult).then_inc(S[f"n{n}_step"], 1)

            def key_reciprocal(b, half):
                dve.wait_ge(S["k_dev"], at(2 * b + half + 1))
                v.reciprocal(krd[:, :], kdev[:, :]).then_inc(S["k_rdev"], 1)
                dve.wait_ge(S["k_rdev"], at(2 * b + half + 1))
                v.tensor_copy(krx[:, :, :], krd[:, :].unsqueeze(2).broadcast_to([P, TILES * HH, DK])).then_inc(
                    S["k_spread"], 1)

            def norm_k(b, half):
                dve.wait_ge(S["k_scale"], at(2 * b + half + 1))
                dve.wait_ge(S["qk_done"], at(2 * (b - 1) + half + 1))
                dve.wait_ge(S["hebb_done"], at(SLOTS * (b - 1) + HS * (half + 1)))
                v.tensor_tensor(kf[:, half, :], p_a[:, :], kc[:, :], ALU.mult).then_inc(S["k_done"], 1)

            def own_value(b, half):
                dve.wait_ge(S["own_sum"], at(2 * b + half + 1))
                dve.wait_ge(S["y_done"], at(2 * (b - 1) + half + 1))
                v.tensor_tensor(dv[:, half, :], p_a[:, 0:C], vf[:, half, 0:C], ALU.mult).then_inc(S["dv_done"], 1)

            def add_own(b, half):
                dve.wait_ge(S["y_copied"], at(2 * b + half + 1))
                dve.wait_ge(S["dv_done"], at(2 * b + half + 1))
                v.tensor_tensor(yt[:, half, 0:C], yt[:, half, 0:C], dv[:, half, :], ALU.add).then_inc(S["y_done"], 1)

            def hebbian(b, s):
                dve.wait_ge(S["rep_done"], at(SLOTS * b + s + 1))
                dve.wait_ge(S["pair_done"], at(2 * (SLOTS * b + s - 1)))
                if s % HS == 0:
                    dve.wait_ge(S["k_done"], at(2 * b + s // HS + 1))
                key = kf[:, s // HS, :].unsqueeze(1).broadcast_to([P, 2, L])
                v.tensor_tensor(hebb[:, s % 2, :, :], p_rep[s % 2][:, :, :], key, ALU.mult).then_inc(
                    S["hebb_done"], 1)

            def pairs(b, s):
                half, features = step_features(s)
                dve.wait_ge(S["hebb_done"], at(SLOTS * b + s + 1))
                dve.wait_ge(S["state_done"], at(SLOTS * b + s - 1))
                for i, d in enumerate(features):
                    r = half * DK + d
                    v.scalar_tensor_tensor(pair[:, s % 2, i, :], hebb[:, s % 2, i, 0:C], ret[:, r:r + 1],
                                           hebb[:, s % 2, i, C:L], ALU.mult, ALU.add).then_inc(S["pair_done"], 1)

            def states(b, s):
                half, features = step_features(s)
                dve.wait_ge(S["prod_done"], at(SLOTS * b + s + 1 - NS))
                for i, d in enumerate(features):
                    r = half * DK + d
                    dve.wait_ge(S["pair_done"], at(2 * (SLOTS * b + s) + i + 1))
                    last = v.tensor_tensor_scan(state[:, s % NS, i, 1:C + 1], ret2[:, r:r + 1].broadcast_to([P, C]),
                                                pair[:, s % 2, i, :], 0.0, ALU.mult, ALU.add)
                last.then_inc(S["state_done"], 1)

            def spikes(b, j):
                if j == 0:
                    dve.wait_ge(S["yf_done"], at(TILES * (b + 1)))
                    dve.wait_ge(S["n4_done"], at(TILES * b))
                    v.tensor_scalar(spk[:, :, :], yf[:, :, :], DRIVES[0], None, ALU.is_gt).then_inc(
                        S["spike_step"], 1)
                else:
                    dve.wait_ge(S["spike_step"], at(STEPS * b + j))
                    v.scalar_tensor_tensor(spk[:, :, :], yf[:, :, :], DRIVES[j], spk[:, :, :], ALU.is_gt,
                                           ALU.add).then_inc(S["spike_step"], 1)

            v.memset(eps_sb[:, 0:1], LN_EPS)
            v.memset(eps_sb[:, 1:2], LN_EPS * STEPS ** 2)
            for r in range(NS):
                v.memset(state[:, r, :, 0:1], 0.0)
            step(v.memset(summer[:, :, :, :, :, :], 0.0))
            statistics(1, 0, xa, "x_in", 16)
            dve.wait_ge(S["params_in"], 48)
            step(v.tensor_tensor(gvt[:, :], hp[:, 0, :], hp[:, 1, :], ALU.subtract))
            for half in range(HALVES):
                hs = slice(half * DK, (half + 1) * DK)
                last = v.tensor_scalar(vn[:, hs], wt[:, hs], gvt[:, half:half + 1], None, ALU.add)
            step(last)
            step(v.tensor_scalar(absv[:, :], vn[:, :], -1.0, None, ALU.mult))
            v.tensor_tensor(absv[:, :], absv[:, :], vn[:, :], ALU.max).then_inc(S["setup_ready"], 1)

            dve.wait_ge(S["setup_exp"], 1)
            step(v.tensor_scalar(t0[:, :], zt[:, :], 2.0, None, ALU.add))
            step(v.reciprocal(t0[:, :], t0[:, :]))
            step(v.tensor_tensor(t0[:, :], t0[:, :], zt[:, :], ALU.mult))
            step(v.tensor_tensor(t1[:, :], t0[:, :], t0[:, :], ALU.mult))
            step(v.tensor_scalar(t2[:, :], t1[:, :], 1.0 / 15, None, ALU.mult))
            for n in (13, 11, 9, 7, 5, 3):
                step(v.scalar_tensor_tensor(t2[:, :], t2[:, :], 1.0 / n, t1[:, :], ALU.add, ALU.mult))
            step(v.scalar_tensor_tensor(t2[:, :], t2[:, :], 1.0, t0[:, :], ALU.add, ALU.mult))
            step(v.tensor_scalar(t2[:, :], t2[:, :], 2.0, None, ALU.mult))
            step(v.scalar_tensor_tensor(sp_v[:, :], vn[:, :], 0.0, t2[:, :], ALU.max, ALU.add))
            step(v.reciprocal(rch[:, :], hp[:, 4, :]))
            for half in range(HALVES):
                hs = slice(half * DK, (half + 1) * DK)
                step(v.tensor_scalar(t0[:, hs], sp_v[:, hs], hp[:, 2, half:half + 1], None, ALU.mult))
                v.tensor_scalar(goc[:, hs], t0[:, hs], rch[:, half:half + 1], None, ALU.mult)
                last = v.tensor_scalar(marg[:, hs], t0[:, hs], shp[:, 1:2], shp[:, 0:1], ALU.subtract, ALU.mult)
            last.then_inc(S["setup_ready"], 1)
            scales(1, 0)

            dve.wait_ge(S["tables_in"], 48)
            kw = wqkv_sb[:, :, D:2 * D].rearrange("p t (h e) -> p t h e", e=DK)
            v.tensor_scalar(mean_sb[:, :], mask_sb[:, :], 1.0 / DK, None, ALU.mult)
            for t in range(KT):
                last = v.tensor_reduce(ksum[:, t, :], kw[:, t, :, :], AX.X, ALU.add)
            step(last)
            step(v.tensor_scalar(ksum[:, :, :], ksum[:, :, :], 1.0 / DK, None, ALU.mult))
            for t in range(KT):
                v.tensor_tensor(kw[:, t, :, :], kw[:, t, :, :], ksum[:, t, :].unsqueeze(2).broadcast_to([P, H, DK]),
                                ALU.subtract).then_inc(S["centred"], 1)

            step(v.tensor_scalar(t1[:, :], zt[:, :], 1.0, None, ALU.add))
            step(v.reciprocal(t1[:, :], t1[:, :]))
            step(v.scalar_tensor_tensor(t2[:, :], vn[:, :], 0.0, zt[:, :], ALU.is_ge, ALU.max))
            step(v.tensor_tensor(t1[:, :], t1[:, :], t2[:, :], ALU.mult))
            for half in range(HALVES):
                hs = slice(half * DK, (half + 1) * DK)
                step(v.scalar_tensor_tensor(t0[:, hs], sp_v[:, hs], hp[:, 3, half:half + 1], t1[:, hs], ALU.mult,
                                            ALU.mult))
            dve.wait_ge(S["setup_exp"], 2)
            for half in range(HALVES):
                hs = slice(half * DK, (half + 1) * DK)
                step(v.scalar_tensor_tensor(coef[:, hs], signm[:, hs], hp[:, 5, half:half + 1], t0[:, hs], ALU.mult,
                                            ALU.mult))
            v.tensor_tensor(ret2[:, :], ret[:, :], ret[:, :], ALU.mult)
            step(v.tensor_tensor(coefr[:, :], coef[:, :], ret[:, :], ALU.mult))
            key_reciprocal(0, 0)
            norm_k(0, 0)
            mask = mask_sb[:, :].unsqueeze(1)
            for half in range(HALVES):
                hs = slice(half * DK, (half + 1) * DK)
                for weight, to in ((wt, wblk), (coef, cblk)):
                    v.tensor_tensor(to[:, half, :, :], mask.broadcast_to([P, DK, HH]),
                                    weight[:, hs].unsqueeze(2).broadcast_to([P, DK, HH]), ALU.mult)
                for i, weight in enumerate((coefr, coef)):
                    for dl in range(4):
                        by_group = weight[:, hs].rearrange("p (g l) -> p g l", g=GRP)[:, :, dl]
                        last = v.tensor_tensor(summer[:, i, half, dl, :, dl * HH:(dl + 1) * HH],
                                               mask.broadcast_to([P, GRP, HH]),
                                               by_group.unsqueeze(2).broadcast_to([P, GRP, HH]), ALU.mult)
            last.then_inc(S["tables_done"], 1)
            dve.wait_ge(S["tables_done"], 1)

            def iteration(g, now, before, two_before, after):
                b, b1, b2 = g + 1, g - 1, g - 2
                for s in range(SLOTS):
                    ends = (g, s - 1) if s > 0 else (g - 1, SLOTS - 1)
                    ending = now if s > 0 else before
                    if ending: pairs(*ends)
                    if now: hebbian(g, s)
                    if ending: states(*ends)
                    if now and s == 2: key_reciprocal(g, 1)
                    if after and s == 4: statistics(1, b, xa, "x_in", 16 * (b + 1))
                    if before and s == 4: add_own(b1, 1)
                    if now and s == 5: norm_k(g, 1)
                    if after and s == 5: scales(1, b)
                    if now and s == 6: own_value(g, 0)
                    if before and s == 7: statistics(2, b1, oo, "o_done", 2 * (b1 + 1))
                    if before and s == 8: scales(2, b1)
                    if after and s == 10: key_reciprocal(b, 0)
                    if now and s == 10: own_value(g, 1)
                    if before and s == 10: statistics(3, b1, x1, "x1_done", b1 + 1)
                    if before and s == 11: scales(3, b1)
                    if two_before and s in (10, 11, 12):
                        for j in {10: (0,), 11: (1, 2), 12: (3, 4)}[s]:
                            spikes(b2, j)
                    if now and s == 12: add_own(g, 0)
                    if two_before and s == 12: statistics(4, b2, spk, "spike_step", STEPS * (b2 + 1))
                    if two_before and s == 13: scales(4, b2)
                    if after and s == 13: norm_k(b, 0)

            run(dve, iteration)

        @block.gpsimd
        def _(pool):
            p = nc.gpsimd

            def read(b, s):
                pool.wait_ge(S["state_done"], at(SLOTS * b + s + 1))
                pool.wait_ge(S["sum_done"], at(HS * b + s // 2 - 3))
                if s % HS == 0:
                    pool.wait_ge(S["q_done"], at(2 * b + s // HS + 1))
                for i in range(2):
                    last = p.tensor_tensor(prod[:, s % NZ, :, i * C:(i + 1) * C], state[:, s % NS, :, i:i + C],
                                           qf[:, s // HS, i * C:(i + 1) * C].unsqueeze(1).broadcast_to([P, 2, C]),
                                           ALU.mult)
                last.then_inc(S["prod_done"], 1)

            def query_key(b, half):
                pool.wait_ge(S["k_done"], at(2 * b + half + 1))
                pool.wait_ge(S["q_done"], at(2 * b + half + 1))
                pool.wait_ge(S["dv_done"], at(2 * (b - 1) + half + 1))
                p.tensor_tensor(qk[:, half, :], qf[:, half, 0:C], kf[:, half, 0:C], ALU.mult).then_inc(
                    S["qk_done"], 1)

            def add_attention(b):
                pool.wait_ge(S["n2_done"], at(TILES * (b + 1)))
                pool.wait_ge(S["again_in"], at(16 * (b + 1)))
                pool.wait_ge(S["n3_done"], at(TILES * b))
                pool.wait_ge(S["keep_done"], at(16 * b))
                p.tensor_tensor(x1[:, :, :], on[:, :, :], xr[:, :, :], ALU.add).then_inc(S["x1_done"], 1)

            def add_feed_forward(b):
                pool.wait_ge(S["n4_done"], at(TILES * (b + 1)))
                pool.wait_ge(S["keep_done"], at(16 * (b + 1)))
                pool.wait_ge(S["out_done"], at(16 * b))
                p.tensor_tensor(res[:, :, :], sn[:, :, :], x1k[:, :, :], ALU.add).then_inc(S["res_done"], 1)

            def iteration(g, now, before, two_before, after):
                for s in range(SLOTS):
                    if s > 0 and now: read(g, s - 1)
                    if s == 0 and before: read(g - 1, SLOTS - 1)
                    if now and s == 2: query_key(g, 0)
                    if now and s == 7: query_key(g, 1)
                    if before and s == 9: add_attention(g - 1)
                    if two_before and s == 14: add_feed_forward(g - 2)

            run(pool, iteration)


def constants():
    ident = np.eye(P, dtype=np.float32)
    head_of = np.arange(P) // DK
    head_mask = (head_of[:, None] == np.arange(HH)[None, :]).astype(np.float32)
    pick = np.zeros((P, DK, P), np.float32)
    for d in range(DK):
        pick[d * HH + head_of, d, np.arange(P)] = 1.0
    return ident, head_mask, pick


def kernel(**inputs):
    import concourse.bacc as _bacc
    from concourse import mybir as _mybir
    from concourse.bass_utils import run_bass_kernel_spmd as _run

    a = {k: np.asarray(v) for k, v in inputs.items()}

    def by_value_feature(w):
        return w.reshape(HALVES, HH, DK, -1).transpose(0, 2, 1, 3).reshape(D, -1)

    w_qkv = a["L0_attn_W_qkv"]
    w_qkv = np.concatenate([w_qkv[:2 * D], by_value_feature(w_qkv[2 * D:])]).T
    w_o = by_value_feature(a["L0_attn_W_o"].T)
    w_ltm = a["L0_attn_W_LTM"].reshape(HALVES, HH, DK, DK).transpose(1, 3, 0, 2).reshape(P, HALVES * DK)
    names = ["V_gs", "V_T0", "beta_tau", "beta_gm", "C_ch", "gamma"]
    by_head = np.stack([a["L0_attn_" + n].reshape(HALVES, HH).T for n in names], 1)
    head_params = np.repeat(by_head, DK, 0)
    shared = np.broadcast_to(np.concatenate([a["L0_attn_alpha_ppd"], a["L0_attn_IC_threshold"]])[None], (P, 2))
    ident, head_mask, pick = constants()
    given = {
        "x": a["L0_attn_x"].reshape(B * L, D), "w_qkv": w_qkv, "w_o": w_o, "w_fc": a["L0_ffn_W_fc"].T,
        "w_proj": a["L0_ffn_W_proj"].T, "w_ltm": w_ltm, "head_params": head_params, "shared_params": shared,
        "ident": ident, "head_mask": head_mask, "pick": pick,
    }
    nc = _bacc.Bacc("TRN2", target_bir_lowering=False, num_devices=1)
    arrays, args = {}, []
    for name, value in given.items():
        value = np.ascontiguousarray(value)
        arrays[f"in_{name}"] = value
        args.append(nc.dram_tensor(f"in_{name}", value.shape, _mybir.dt.from_np(value.dtype),
                                   kind="ExternalInput").ap())
    out = nc.dram_tensor("out", (B * L, D), _mybir.dt.float32, kind="ExternalOutput").ap()
    build(nc, *args, out)
    r = _run(nc, [arrays], core_ids=[0])
    return r.results[0]["out"].reshape(B, L, D)
```

```python
from contextlib import ExitStack

import numpy as np

import concourse.bass as bass
from concourse import mybir

F32 = mybir.dt.float32
F32R = mybir.dt.float32r
ALU = mybir.AluOpType
ACT = mybir.ActivationFunctionType
AX = mybir.AxisListType

B, L, D, H, DK, F = 8, 512, 256, 16, 16, 1024
P = 128
KT = D // P
HALVES = KT
HH = H // HALVES
TILES = L // P
FT = F // P
GRP = 4
SLOTS = 16
HS = SLOTS // HALVES
NS = 4
NZ = 8
LN_EPS = 1e-5
STEPS, BETA, THRESHOLD = 5, 0.9, 1.0


def spike_count(y):
    mem, spikes = np.float32(0), 0
    for _ in range(STEPS):
        reset = np.float32(mem - np.float32(THRESHOLD) > 0)
        mem = np.float32(np.float32(BETA) * mem + y) - reset * np.float32(THRESHOLD)
        spikes += int(mem - np.float32(THRESHOLD) > 0)
    return spikes


def spike_drives():
    out = []
    for k in range(1, STEPS + 1):
        low, high = np.float32(0), np.float32(2)
        while np.nextafter(low, high, dtype=np.float32) < high:
            mid = np.float32((low + high) / 2)
            low, high = (mid, high) if spike_count(mid) < k else (low, mid)
        out.append(float(low))
    return out


DRIVES = spike_drives()


def step_features(s):
    j = s % HS
    first = j // 2 + 8 * (j % 2)
    return s // HS, (first, first + 4)


def build(nc, x, w_qkv, w_o, w_fc, w_proj, w_ltm, head_params, shared_params, ident, head_mask, pick, out):
    ctx = ExitStack()
    with ctx:
        def sb(name, shape, dt=F32):
            return ctx.enter_context(nc.sbuf_tensor(name, shape, dt))

        def ps(name, shape):
            return ctx.enter_context(nc.psum_tensor(name, shape, F32))

        def sem(name):
            return ctx.enter_context(nc.semaphore(name))

        wqkv_sb = sb("wqkv_sb", [P, KT, 3 * D])
        wo_sb = sb("wo_sb", [P, HALVES, D])
        wfc_sb = sb("wfc_sb", [P, KT, F])
        wproj_sb = sb("wproj_sb", [P, FT, D])
        pick_sb = sb("pick_sb", [P, DK, P], F32R)
        ident_sb = sb("ident_sb", [P, P])
        mask_sb = sb("mask_sb", [P, HH])
        mean_sb = sb("mean_sb", [P, HH])
        wt = sb("wt", [P, HALVES * DK])
        hp = sb("hp", [P, 6, HALVES])
        shp = sb("shp", [P, 2])
        vn = sb("vn", [P, HALVES * DK])
        absv, zt, goc, marg, signm, sp_v, t0, t1, t2 = (
            sb(name, [P, HALVES * DK]) for name in "absv zt goc marg signm sp_v t0 t1 t2".split())
        gvt = sb("gvt", [P, HALVES])
        rch = sb("rch", [P, HALVES])
        ret = sb("ret", [P, HALVES * DK])
        coef = sb("coef", [P, HALVES * DK])
        wblk = sb("wblk", [P, HALVES, DK, HH])
        summer = sb("summer", [P, HALVES, 4, GRP, 4 * HH])
        eps_sb = sb("eps_sb", [P, 2])
        ksum = sb("ksum", [P, KT, H])

        stats = [sb(f"stats{i}", [P, TILES, 6]) for i in range(4)]
        moments = [sb(f"moments{i}", [P, 3, TILES]) for i in range(4)]
        dev = [sb(f"dev{i}", [P, TILES]) for i in range(4)]
        rdev = [sb(f"rdev{i}", [P, TILES]) for i in range(4)]
        nmr = [sb(f"nmr{i}", [P, TILES]) for i in range(4)]

        xa = sb("xa", [P, TILES, D])
        xr = sb("xr", [P, TILES, D])
        xn = sb("xn", [P, TILES, D])
        xt = sb("xt", [P, KT, L])
        kc = sb("kc", [P, L])
        ksq = sb("ksq", [P, L])
        kdev = sb("kdev", [P, TILES * HH])
        krd = sb("krd", [P, TILES * HH])
        krx = sb("krx", [P, TILES * HH, DK])
        kf = sb("kf", [P, HALVES, L])
        qf = sb("qf", [P, HALVES, L])
        vf = sb("vf", [P, HALVES, L])
        vh = sb("vh", [P, HALVES, L], F32R)
        vl = sb("vl", [P, HALVES, L], F32R)
        hebb = sb("hebb", [P, 2, 2, L])
        state = sb("state", [P, NS, 2, L])
        prod = sb("prod", [P, NZ, 2, L])
        yt = sb("yt", [P, HALVES, L])
        oo = sb("oo", [P, TILES, D])
        x1 = sb("x1", [P, TILES, D])
        x1k = sb("x1k", [P, TILES, D])
        x1n = sb("x1n", [P, TILES, D])
        x1t = sb("x1t", [P, KT, L])
        hr = sb("hr", [P, 2, L])
        ht = sb("ht", [P, FT, L])
        yf = sb("yf", [P, TILES, D])
        spk = sb("spk", [P, TILES, D])
        res = sb("res", [P, TILES, D])

        p_rep = [ps(f"p_rep{i}", [P, 2, L]) for i in range(2)]
        p_y = [ps(f"p_y{i}", [P, L]) for i in range(HALVES)]
        p_a = ps("p_a", [P, L])
        p_c = ps("p_c", [P, L])

        S = {name: sem(name) for name in """
            x_in params_in tables_in weights_in again_in out_done keep_done
            setup_ready setup_exp centred tables_done setup_step
            n1_stats n1_diff n1_var n1_dev n1_step n1_done  xt_turned xt_done
            k_proj k_sq k_var k_dev k_rdev k_spread k_scale k_done  v_proj v_done  q_proj q_done
            pick_in v_high v_low
            rep_done hebb_done state_done prod_done sum_done y_done
            o_proj o_done n2_stats n2_diff n2_var n2_dev n2_step n2_done x1_done
            n3_stats n3_diff n3_var n3_dev n3_step n3_done  x1_turned x1t_done
            up_done relu_done h_done down_done yf_done
            spike_step n4_stats n4_diff n4_var n4_dev n4_step n4_done res_done""".split()}

        def at(value):
            return max(value, 0) if isinstance(value, int) else value

        def run(eng, iteration):
            iteration(0, True, False, False, True)
            iteration(1, True, True, False, True)
            with eng.Fori(2, B - 1) as g:
                iteration(g, True, True, True, True)
            iteration(B - 1, True, True, True, False)
            iteration(B, False, True, True, False)
            iteration(B + 1, False, False, True, False)

        def tokens(u):
            return slice(u * P, (u + 1) * P)

        def by_tile(a, b):
            return a[bass.ds(b * L, L), :].rearrange("(u p) d -> p u d", p=P)

        block = ctx.enter_context(nc.Block())

        @block.sync
        def _(sp):
            sp.dma_start(xa[:, :, :], by_tile(x, 0)).then_inc(S["x_in"], 16)
            sp.dma_start(ident_sb[:, :], ident).then_inc(S["tables_in"], 16)
            sp.dma_start(wqkv_sb[:, :, :], w_qkv.rearrange("(t p) n -> p t n", p=P)).then_inc(S["tables_in"], 16)
            sp.dma_start(mask_sb[:, :], head_mask).then_inc(S["tables_in"], 16)
            sp.dma_start(wt[:, :], w_ltm).then_inc(S["params_in"], 16)
            sp.dma_start(hp[:, :, :], head_params).then_inc(S["params_in"], 16)
            sp.dma_start(shp[:, :], shared_params).then_inc(S["params_in"], 16)
            sp.dma_start(wo_sb[:, :, :], w_o.rearrange("(t p) n -> p t n", p=P)).then_inc(S["weights_in"], 16)
            sp.dma_start(wfc_sb[:, :, :], w_fc.rearrange("(t p) n -> p t n", p=P)).then_inc(S["weights_in"], 16)
            sp.dma_start(wproj_sb[:, :, :], w_proj.rearrange("(t p) n -> p t n", p=P)).then_inc(S["weights_in"], 16)

            def iteration(g, now, before, two_before, after):
                if after:
                    sp.wait_ge(S["n1_done"], at(TILES * (g + 1)))
                    sp.dma_start(xa[:, :, :], by_tile(x, g + 1)).then_inc(S["x_in"], 16)
                if before:
                    sp.wait_ge(S["x1_done"], at(g - 1))
                    sp.dma_start(xr[:, :, :], by_tile(x, g - 1)).then_inc(S["again_in"], 16)
                if two_before:
                    sp.wait_ge(S["res_done"], at(g - 1))
                    sp.dma_start(by_tile(out, g - 2), res[:, :, :]).then_inc(S["out_done"], 16)
                if before:
                    sp.wait_ge(S["x1_done"], at(g))
                    sp.dma_start(x1k[:, :, :], x1[:, :, :]).then_inc(S["keep_done"], 16)

            run(sp, iteration)
            sp.wait_ge(S["out_done"], at(16 * B))

        @block.tensor
        def _(pe):
            def turn_x(b, t):
                pe.wait_ge(S["k_done"], at(2 * b))
                pe.wait_ge(S["xt_done"], at(KT * b + t))
                pe.wait_ge(S["n1_done"], at(TILES * (b + 1)))
                for u in range(TILES):
                    last = pe.transpose(p_a[:, tokens(u)], xn[:, u, t * P:(t + 1) * P], ident_sb[:, :])
                last.then_inc(S["xt_turned"], 1)

            def project(b, first_col, done):
                for t in range(KT):
                    last = pe.matmul(p_a[:, :], wqkv_sb[:, t, first_col:first_col + P], xt[:, t, :],
                                     start=(t == 0), stop=(t == KT - 1))
                last.then_inc(S[done], 1)

            def project_k(b, half):
                pe.wait_ge(S["xt_done"], at(KT * (b + 1)))
                pe.wait_ge(S["k_done"], at(2 * b + half))
                project(b, D + half * P, "k_proj")

            def project_v(b, half):
                pe.wait_ge(S["k_dev"], at(2 * b + half + 1))
                project(b, 2 * D + half * P, "v_proj")

            def project_q(b, half):
                pe.wait_ge(S["v_done"], at(2 * b + half + 1))
                project(b, half * P, "q_proj")

            def key_variance(b, half):
                pe.wait_ge(S["k_sq"], at(2 * b + half + 1))
                for u in range(TILES):
                    last = pe.matmul(p_a[:, u * HH:(u + 1) * HH], ksq[:, u * P:(u + 1) * P], mean_sb[:, :],
                                     start=True, stop=True)
                last.then_inc(S["k_var"], 1)

            def key_scale(b, half):
                pe.wait_ge(S["k_spread"], at(2 * b + half + 1))
                pe.wait_ge(S["q_done"], at(2 * b + half + 1))
                for u in range(TILES):
                    scale = krx[:, u * HH:(u + 1) * HH, :].rearrange("p h e -> p (h e)")
                    last = pe.transpose(p_a[:, tokens(u)], scale, ident_sb[:, :])
                last.then_inc(S["k_scale"], 1)

            def replicate(b, s):
                half, features = step_features(s)
                pe.wait_ge(S["hebb_done"], at(SLOTS * b + s - 1))
                if s % HS == 0:
                    pe.wait_ge(S["v_low"], at(2 * b + half + 1))
                for i, d in enumerate(features):
                    pe.matmul(p_rep[s % 2][:, i, :], pick_sb[:, d, :], vh[:, half, :], start=True, stop=False)
                    last = pe.matmul(p_rep[s % 2][:, i, :], pick_sb[:, d, :], vl[:, half, :], start=False, stop=True)
                last.then_inc(S["rep_done"], 1)

            def sums(b, m):
                half, dl = m // 4, m % 4
                if dl == 0:
                    pe.wait_ge(S["y_done"], at(2 * (b - 1) + half + 1))
                    pe.wait_ge(S["q_done"], at(2 * b + half + 1))
                    pe.matmul(p_y[half][:, :], wblk[:, half, :, :].rearrange("p d h -> p (d h)"), qf[:, half, :],
                              start=True, stop=False, skip_group_check=True)
                pe.wait_ge(S["prod_done"], at(SLOTS * b + 2 * m + 2))
                for grp in range(GRP):
                    s = 2 * m + grp // 2
                    last = pe.matmul(p_y[half][32 * grp:32 * grp + 32, :], summer[:, half, dl, grp, :],
                                     prod[:, s % NZ, grp % 2, :], start=False, stop=(dl == 3),
                                     skip_group_check=True)
                last.then_inc(S["sum_done"], 1)

            def project_out(b, t):
                pe.wait_ge(S["relu_done"], at(FT * b))
                pe.wait_ge(S["o_done"], at(2 * b + t))
                pe.wait_ge(S["y_done"], at(2 * (b + 1)))
                for i in range(2):
                    for half in range(HALVES):
                        last = pe.matmul(p_c[:, i * D:(i + 1) * D], yt[:, half, tokens(2 * t + i)], wo_sb[:, half, :],
                                         start=(half == 0), stop=(half == HALVES - 1))
                last.then_inc(S["o_proj"], 1)

            def turn_x1(b, t):
                pe.wait_ge(S["o_done"], at(2 * (b + 1)))
                pe.wait_ge(S["yf_done"], at(TILES * b))
                pe.wait_ge(S["x1t_done"], at(KT * b + t))
                pe.wait_ge(S["n3_done"], at(TILES * (b + 1)))
                for u in range(TILES):
                    last = pe.transpose(p_c[:, tokens(u)], x1n[:, u, t * P:(t + 1) * P], ident_sb[:, :])
                last.then_inc(S["x1_turned"], 1)

            def up(b, f):
                pe.wait_ge(S["x1t_done"], at(KT * (b + 1)))
                pe.wait_ge(S["relu_done"], at(FT * b + f))
                for t in range(KT):
                    last = pe.matmul(p_c[:, :], wfc_sb[:, t, f * P:(f + 1) * P], x1t[:, t, :],
                                     start=(t == 0), stop=(t == KT - 1))
                last.then_inc(S["up_done"], 1)

            def down(b, u, next_too):
                pe.wait_ge(S["h_done"], at(FT * (b + 1)))
                if next_too:
                    pe.wait_ge(S["o_done"], at(2 * (b + 2)))
                pe.wait_ge(S["yf_done"], at(TILES * b + u))
                for f in range(FT):
                    last = pe.matmul(p_c[:, 0:D], ht[:, f, u * P:(u + 1) * P], wproj_sb[:, f, :],
                                     start=(f == 0), stop=(f == FT - 1))
                last.then_inc(S["down_done"], 1)

            pe.wait_ge(S["tables_in"], 48)
            turn_x(0, 0)
            turn_x(0, 1)
            pe.wait_ge(S["centred"], 2)
            project_k(0, 0)
            key_variance(0, 0)
            project_v(0, 0)
            project_q(0, 0)
            key_scale(0, 0)
            pe.wait_ge(S["weights_in"], 48)
            pe.wait_ge(S["pick_in"], 16)
            replicate(0, 0)
            pe.wait_ge(S["tables_done"], 1)

            def iteration(g, now, before, two_before, after):
                for s in range(SLOTS):
                    if now and s < SLOTS - 1:
                        replicate(g, s + 1)
                    if now:
                        if s == 0: project_k(g, 1)
                        if s == 1: key_variance(g, 1)
                        if s == 2: project_v(g, 1)
                        if s == 3: project_q(g, 1)
                        if s == 4: key_scale(g, 1)
                    if two_before and s < 5:
                        up(g - 2, 3 + s)
                    if before and s == 6:
                        project_out(g - 1, 0)
                        project_out(g - 1, 1)
                    if after:
                        if s == 7: turn_x(g + 1, 0)
                        if s == 7: turn_x(g + 1, 1)
                        if s == 8: project_k(g + 1, 0)
                        if s == 9: key_variance(g + 1, 0)
                    if after:
                        if s == 10: project_v(g + 1, 0)
                        if s == 11: project_q(g + 1, 0)
                        if s == 13: key_scale(g + 1, 0)
                    if two_before and 7 <= s < 7 + TILES:
                        down(g - 2, s - 7, before)
                    if before and s == 12:
                        turn_x1(g - 1, 0)
                        turn_x1(g - 1, 1)
                    if before and s >= 13:
                        up(g - 1, s - 13)
                    if before and s in (1, 3):
                        sums(g - 1, 6 + s // 2)
                    if now and s >= 5 and s % 2:
                        sums(g, (s - 5) // 2)
                    if after and s == SLOTS - 1:
                        replicate(g + 1, 0)

            run(pe, iteration)

        @block.scalar
        def _(act):
            act.wait_ge(S["setup_ready"], 1)
            nc.scalar.activation(zt[:, :], absv[:, :], ACT.Exp, scale=-1.0).then_inc(S["setup_exp"], 1)
            act.wait_ge(S["setup_ready"], 2)
            nc.scalar.activation(ret[:, :], goc[:, :], ACT.Exp, scale=-1.0)
            nc.scalar.activation(signm[:, :], marg[:, :], ACT.Tanh).then_inc(S["setup_exp"], 1)

            def deviation(n, b):
                act.wait_ge(S[f"n{n}_var"], at(b + 1))
                eps = eps_sb[:, 1:2] if n == 4 else eps_sb[:, 0:1]
                nc.scalar.activation(dev[n - 1][:, :], moments[n - 1][:, 2, :], ACT.Sqrt, bias=eps,
                                     scale=1.0 / D).then_inc(S[f"n{n}_dev"], 1)

            def norm(n, b, src, dst, used, count):
                act.wait_ge(S[f"n{n}_step"], at(2 * (b + 1)))
                act.wait_ge(S[used], at(count))
                for u in range(TILES):
                    nc.scalar.activation(dst[:, u, :], src[:, u, :], ACT.Identity, scale=rdev[n - 1][:, u:u + 1],
                                         bias=nmr[n - 1][:, u:u + 1]).then_inc(S[f"n{n}_done"], 1)

            def copy(src, dst, ready, count, done):
                act.wait_ge(S[ready], at(count))
                nc.scalar.copy(dst, src).then_inc(S[done], 1)

            def norm1(b):
                norm(1, b, xa, xn, "xt_turned", KT * b)

            def copy_xt(b):
                for t in range(KT):
                    copy(p_a[:, :], xt[:, t, :], "xt_turned", KT * b + t + 1, "xt_done")

            def square_k(b, half):
                act.wait_ge(S["k_proj"], at(2 * b + half + 1))
                act.wait_ge(S["k_done"], at(2 * b + half))
                nc.scalar.copy(kc[:, :], p_a[:, :])
                nc.scalar.activation(ksq[:, :], p_a[:, :], ACT.Square).then_inc(S["k_sq"], 1)

            def key_deviation(b, half):
                act.wait_ge(S["k_var"], at(2 * b + half + 1))
                nc.scalar.activation(kdev[:, :], p_a[:, 0:TILES * HH], ACT.Sqrt, bias=eps_sb[:, 0:1]).then_inc(
                    S["k_dev"], 1)

            def copy_v(b, half):
                copy(p_a[:, :], vf[:, half, :], "v_proj", 2 * b + half + 1, "v_done")
                copy(vf[:, half, :], vh[:, half, :], "v_done", 2 * b + half + 1, "v_high")

            def copy_q(b, half):
                act.wait_ge(S["prod_done"], at(SLOTS * (b - 1) + HS * (half + 1)))
                copy(p_a[:, :], qf[:, half, :], "q_proj", 2 * b + half + 1, "q_done")

            def copy_y(b, half):
                act.wait_ge(S["o_proj"], at(2 * b))
                copy(p_y[half][:, :], yt[:, half, :], "sum_done", HS * b + 4 * (half + 1), "y_done")

            def copy_o(b, t):
                act.wait_ge(S["x1_done"], at(b))
                copy(p_c[:, :], oo[:, 2 * t:2 * t + 2, :].rearrange("p u d -> p (u d)"), "o_proj", 2 * b + t + 1,
                     "o_done")

            def copy_x1t(b):
                for t in range(KT):
                    copy(p_c[:, :], x1t[:, t, :], "x1_turned", KT * b + t + 1, "x1t_done")

            def hidden(b, f):
                act.wait_ge(S["up_done"], at(FT * b + f + 1))
                act.wait_ge(S["h_done"], at(FT * b + f - 1))
                nc.scalar.activation(hr[:, f % 2, :], p_c[:, :], ACT.Relu).then_inc(S["relu_done"], 1)
                act.wait_ge(S["relu_done"], at(FT * b + f + 1))
                nc.scalar.activation(ht[:, f, :], hr[:, f % 2, :], ACT.Square).then_inc(S["h_done"], 1)

            def copy_yf(b, u):
                act.wait_ge(S["spike_step"], at(STEPS * b))
                copy(p_c[:, 0:D], yf[:, u, :], "down_done", TILES * b + u + 1, "yf_done")

            deviation(1, 0)
            norm1(0)
            copy_xt(0)
            square_k(0, 0)
            key_deviation(0, 0)
            copy_v(0, 0)
            copy_q(0, 0)

            def iteration(g, now, before, two_before, after):
                b, b1, b2 = g + 1, g - 1, g - 2
                for s in range(SLOTS):
                    if now:
                        if s == 0: square_k(g, 1)
                        if s == 1: key_deviation(g, 1)
                        if s == 2: copy_v(g, 1)
                        if s == 3: copy_q(g, 1)
                    if before and s == 4: copy_y(b1, 1)
                    if two_before and s < 5: hidden(b2, 3 + s)
                    if after and s == 4: deviation(1, b)
                    if after and s == 5: norm1(b)
                    if before and s == 6:
                        copy_o(b1, 0)
                        copy_o(b1, 1)
                    if after and s == 7: copy_xt(b)
                    if before and s == 8:
                        deviation(2, b1)
                        norm(2, b1, oo, oo, "x1_done", b1)
                    if after and s == 8: square_k(b, 0)
                    if after and s == 9: key_deviation(b, 0)
                    if two_before and 7 <= s < 7 + TILES: copy_yf(b2, s - 7)
                    if after and s == 10: copy_v(b, 0)
                    if before and s == 11:
                        deviation(3, b1)
                        norm(3, b1, x1, x1n, "x1_turned", KT * b1)
                    if after and s == 11: copy_q(b, 0)
                    if now and s == 12: copy_y(g, 0)
                    if before and s == 12: copy_x1t(b1)
                    if two_before and s == 13:
                        deviation(4, b2)
                        norm(4, b2, spk, spk, "res_done", b2)
                    if before and s >= 13: hidden(b1, s - 13)

            run(act, iteration)

        @block.vector
        def _(dve):
            v = nc.vector
            steps = [0]

            def step(ins):
                steps[0] += 1
                ins.then_inc(S["setup_step"], 1)
                dve.wait_ge(S["setup_step"], steps[0])

            def statistics(n, b, src, ready, count):
                dve.wait_ge(S[ready], at(count))
                dve.wait_ge(S[f"n{n}_var"], at(b))
                for u in range(TILES):
                    last = v.bn_stats(stats[n - 1][:, u, :], src[:, u, :])
                last.then_inc(S[f"n{n}_stats"], 1)
                dve.wait_ge(S[f"n{n}_stats"], at(b + 1))
                dve.wait_ge(S[f"n{n}_step"], at(2 * b))
                st, mo = stats[n - 1], moments[n - 1]
                v.tensor_tensor(mo[:, 0, :], st[:, :, 1], st[:, :, 4], ALU.add)
                v.tensor_tensor(mo[:, 1, :], st[:, :, 1], st[:, :, 4], ALU.subtract).then_inc(S[f"n{n}_diff"], 1)
                v.tensor_tensor(mo[:, 2, :], st[:, :, 2], st[:, :, 5], ALU.add).then_inc(S[f"n{n}_diff"], 1)
                dve.wait_ge(S[f"n{n}_diff"], at(3 * b + 1))
                v.scalar_tensor_tensor(mo[:, 1, :], mo[:, 1, :], D / 4, mo[:, 1, :], ALU.mult, ALU.mult).then_inc(
                    S[f"n{n}_diff"], 1)
                dve.wait_ge(S[f"n{n}_diff"], at(3 * (b + 1)))
                v.tensor_tensor(mo[:, 2, :], mo[:, 2, :], mo[:, 1, :], ALU.add).then_inc(S[f"n{n}_var"], 1)

            def scales(n, b):
                dve.wait_ge(S[f"n{n}_dev"], at(b + 1))
                dve.wait_ge(S[f"n{n}_done"], at(TILES * b))
                v.reciprocal(rdev[n - 1][:, :], dev[n - 1][:, :]).then_inc(S[f"n{n}_step"], 1)
                dve.wait_ge(S[f"n{n}_step"], at(2 * b + 1))
                v.scalar_tensor_tensor(nmr[n - 1][:, :], moments[n - 1][:, 0, :], -0.5, rdev[n - 1][:, :], ALU.mult,
                                       ALU.mult).then_inc(S[f"n{n}_step"], 1)

            def key_reciprocal(b, half):
                dve.wait_ge(S["k_dev"], at(2 * b + half + 1))
                v.reciprocal(krd[:, :], kdev[:, :]).then_inc(S["k_rdev"], 1)
                dve.wait_ge(S["k_rdev"], at(2 * b + half + 1))
                v.tensor_copy(krx[:, :, :], krd[:, :].unsqueeze(2).broadcast_to([P, TILES * HH, DK])).then_inc(
                    S["k_spread"], 1)

            def norm_k(b, half):
                dve.wait_ge(S["k_scale"], at(2 * b + half + 1))
                dve.wait_ge(S["hebb_done"], at(SLOTS * (b - 1) + HS * (half + 1)))
                v.tensor_tensor(kf[:, half, :], p_a[:, :], kc[:, :], ALU.mult).then_inc(S["k_done"], 1)

            def low_v(b, half):
                dve.wait_ge(S["v_high"], at(2 * b + half + 1))
                v.tensor_tensor(vl[:, half, :], vf[:, half, :], vh[:, half, :].bitcast(F32), ALU.subtract).then_inc(
                    S["v_low"], 1)

            def hebbian(b, s):
                dve.wait_ge(S["rep_done"], at(SLOTS * b + s + 1))
                dve.wait_ge(S["state_done"], at(2 * (SLOTS * b + s - 1)))
                if s % HS == 0:
                    dve.wait_ge(S["k_done"], at(2 * b + s // HS + 1))
                key = kf[:, s // HS, :].unsqueeze(1).broadcast_to([P, 2, L])
                v.tensor_tensor(hebb[:, s % 2, :, :], p_rep[s % 2][:, :, :], key, ALU.mult).then_inc(
                    S["hebb_done"], 1)

            def states(b, s):
                half, features = step_features(s)
                dve.wait_ge(S["hebb_done"], at(SLOTS * b + s + 1))
                dve.wait_ge(S["prod_done"], at(SLOTS * b + s + 1 - NS))
                for i, d in enumerate(features):
                    r = half * DK + d
                    v.tensor_tensor_scan(state[:, s % NS, i, :], ret[:, r:r + 1].broadcast_to([P, L]),
                                         hebb[:, s % 2, i, :], 0.0, ALU.mult, ALU.add).then_inc(S["state_done"], 1)

            def spikes(b, j):
                if j == 0:
                    dve.wait_ge(S["yf_done"], at(TILES * (b + 1)))
                    dve.wait_ge(S["res_done"], at(b))
                    v.tensor_scalar(spk[:, :, :], yf[:, :, :], DRIVES[0], None, ALU.is_gt).then_inc(
                        S["spike_step"], 1)
                else:
                    dve.wait_ge(S["spike_step"], at(STEPS * b + j))
                    v.scalar_tensor_tensor(spk[:, :, :], yf[:, :, :], DRIVES[j], spk[:, :, :], ALU.is_gt,
                                           ALU.add).then_inc(S["spike_step"], 1)

            v.memset(eps_sb[:, 0:1], LN_EPS)
            v.memset(eps_sb[:, 1:2], LN_EPS * STEPS ** 2)
            step(v.memset(summer[:, :, :, :, :], 0.0))
            statistics(1, 0, xa, "x_in", 16)
            dve.wait_ge(S["params_in"], 48)
            step(v.tensor_tensor(gvt[:, :], hp[:, 0, :], hp[:, 1, :], ALU.subtract))
            for half in range(HALVES):
                hs = slice(half * DK, (half + 1) * DK)
                last = v.tensor_scalar(vn[:, hs], wt[:, hs], gvt[:, half:half + 1], None, ALU.add)
            step(last)
            step(v.tensor_scalar(absv[:, :], vn[:, :], -1.0, None, ALU.mult))
            v.tensor_tensor(absv[:, :], absv[:, :], vn[:, :], ALU.max).then_inc(S["setup_ready"], 1)

            dve.wait_ge(S["setup_exp"], 1)
            step(v.tensor_scalar(t0[:, :], zt[:, :], 2.0, None, ALU.add))
            step(v.reciprocal(t0[:, :], t0[:, :]))
            step(v.tensor_tensor(t0[:, :], t0[:, :], zt[:, :], ALU.mult))
            step(v.tensor_tensor(t1[:, :], t0[:, :], t0[:, :], ALU.mult))
            step(v.tensor_scalar(t2[:, :], t1[:, :], 1.0 / 15, None, ALU.mult))
            for n in (13, 11, 9, 7, 5, 3):
                step(v.scalar_tensor_tensor(t2[:, :], t2[:, :], 1.0 / n, t1[:, :], ALU.add, ALU.mult))
            step(v.scalar_tensor_tensor(t2[:, :], t2[:, :], 1.0, t0[:, :], ALU.add, ALU.mult))
            step(v.tensor_scalar(t2[:, :], t2[:, :], 2.0, None, ALU.mult))
            step(v.scalar_tensor_tensor(sp_v[:, :], vn[:, :], 0.0, t2[:, :], ALU.max, ALU.add))
            step(v.reciprocal(rch[:, :], hp[:, 4, :]))
            for half in range(HALVES):
                hs = slice(half * DK, (half + 1) * DK)
                step(v.tensor_scalar(t0[:, hs], sp_v[:, hs], hp[:, 2, half:half + 1], None, ALU.mult))
                v.tensor_scalar(goc[:, hs], t0[:, hs], rch[:, half:half + 1], None, ALU.mult)
                last = v.tensor_scalar(marg[:, hs], t0[:, hs], shp[:, 1:2], shp[:, 0:1], ALU.subtract, ALU.mult)
            last.then_inc(S["setup_ready"], 1)
            scales(1, 0)

            dve.wait_ge(S["tables_in"], 48)
            kw = wqkv_sb[:, :, D:2 * D].rearrange("p t (h e) -> p t h e", e=DK)
            v.tensor_scalar(mean_sb[:, :], mask_sb[:, :], 1.0 / DK, None, ALU.mult)
            for t in range(KT):
                last = v.tensor_reduce(ksum[:, t, :], kw[:, t, :, :], AX.X, ALU.add)
            step(last)
            step(v.tensor_scalar(ksum[:, :, :], ksum[:, :, :], 1.0 / DK, None, ALU.mult))
            for t in range(KT):
                v.tensor_tensor(kw[:, t, :, :], kw[:, t, :, :], ksum[:, t, :].unsqueeze(2).broadcast_to([P, H, DK]),
                                ALU.subtract).then_inc(S["centred"], 1)

            step(v.tensor_scalar(t1[:, :], zt[:, :], 1.0, None, ALU.add))
            step(v.reciprocal(t1[:, :], t1[:, :]))
            step(v.scalar_tensor_tensor(t2[:, :], vn[:, :], 0.0, zt[:, :], ALU.is_ge, ALU.max))
            step(v.tensor_tensor(t1[:, :], t1[:, :], t2[:, :], ALU.mult))
            for half in range(HALVES):
                hs = slice(half * DK, (half + 1) * DK)
                step(v.scalar_tensor_tensor(t0[:, hs], sp_v[:, hs], hp[:, 3, half:half + 1], t1[:, hs], ALU.mult,
                                            ALU.mult))
            dve.wait_ge(S["setup_exp"], 2)
            for half in range(HALVES):
                hs = slice(half * DK, (half + 1) * DK)
                step(v.scalar_tensor_tensor(coef[:, hs], signm[:, hs], hp[:, 5, half:half + 1], t0[:, hs], ALU.mult,
                                            ALU.mult))
            key_reciprocal(0, 0)
            low_v(0, 0)
            norm_k(0, 0)
            mask = mask_sb[:, :].unsqueeze(1)
            for half in range(HALVES):
                hs = slice(half * DK, (half + 1) * DK)
                v.tensor_tensor(wblk[:, half, :, :], mask.broadcast_to([P, DK, HH]),
                                wt[:, hs].unsqueeze(2).broadcast_to([P, DK, HH]), ALU.mult)
                for dl in range(4):
                    by_group = coef[:, hs].rearrange("p (g l) -> p g l", g=GRP)[:, :, dl]
                    last = v.tensor_tensor(summer[:, half, dl, :, dl * HH:(dl + 1) * HH],
                                           mask.broadcast_to([P, GRP, HH]),
                                           by_group.unsqueeze(2).broadcast_to([P, GRP, HH]), ALU.mult)
            last.then_inc(S["tables_done"], 1)
            dve.wait_ge(S["tables_done"], 1)

            def iteration(g, now, before, two_before, after):
                b, b1, b2 = g + 1, g - 1, g - 2
                for s in range(SLOTS):
                    ends = (g, s - 1) if s > 0 else (g - 1, SLOTS - 1)
                    ending = now if s > 0 else before
                    if now: hebbian(g, s)
                    if ending: states(*ends)
                    if now and s == 2: key_reciprocal(g, 1)
                    if after and s == 4: statistics(1, b, xa, "x_in", 16 * (b + 1))
                    if now and s == 3: low_v(g, 1)
                    if now and s == 5: norm_k(g, 1)
                    if after and s == 5: scales(1, b)
                    if before and s == 7: statistics(2, b1, oo, "o_done", 2 * (b1 + 1))
                    if before and s == 8: scales(2, b1)
                    if after and s == 10: key_reciprocal(b, 0)
                    if after and s == 11: low_v(b, 0)
                    if before and s == 10: statistics(3, b1, x1, "x1_done", b1 + 1)
                    if before and s == 11: scales(3, b1)
                    if two_before and s in (10, 11, 12):
                        for j in {10: (0,), 11: (1, 2), 12: (3, 4)}[s]:
                            spikes(b2, j)
                    if two_before and s == 12: statistics(4, b2, spk, "spike_step", STEPS * (b2 + 1))
                    if two_before and s == 13: scales(4, b2)
                    if after and s == 13: norm_k(b, 0)

            run(dve, iteration)

        @block.gpsimd
        def _(pool):
            p = nc.gpsimd

            def read(b, s):
                pool.wait_ge(S["state_done"], at(2 * (SLOTS * b + s + 1)))
                pool.wait_ge(S["sum_done"], at(HS * b + s // 2 - 3))
                if s % HS == 0:
                    pool.wait_ge(S["q_done"], at(2 * b + s // HS + 1))
                p.tensor_tensor(prod[:, s % NZ, :, :], state[:, s % NS, :, :],
                                qf[:, s // HS, :].unsqueeze(1).broadcast_to([P, 2, L]), ALU.mult).then_inc(
                    S["prod_done"], 1)

            def add_attention(b):
                pool.wait_ge(S["n2_done"], at(TILES * (b + 1)))
                pool.wait_ge(S["again_in"], at(16 * (b + 1)))
                pool.wait_ge(S["n3_done"], at(TILES * b))
                pool.wait_ge(S["keep_done"], at(16 * b))
                p.tensor_tensor(x1[:, :, :], oo[:, :, :], xr[:, :, :], ALU.add).then_inc(S["x1_done"], 1)

            def add_feed_forward(b):
                pool.wait_ge(S["n4_done"], at(TILES * (b + 1)))
                pool.wait_ge(S["keep_done"], at(16 * (b + 1)))
                pool.wait_ge(S["out_done"], at(16 * b))
                p.tensor_tensor(res[:, :, :], spk[:, :, :], x1k[:, :, :], ALU.add).then_inc(S["res_done"], 1)

            def iteration(g, now, before, two_before, after):
                for s in range(SLOTS):
                    if s > 0 and now: read(g, s - 1)
                    if s == 0 and before: read(g - 1, SLOTS - 1)
                    if before and s == 9: add_attention(g - 1)
                    if two_before and s == 14: add_feed_forward(g - 2)

            p.dma_start(pick_sb[:, :, :], pick).then_inc(S["pick_in"], 16)
            run(pool, iteration)


def constants():
    ident = np.eye(P, dtype=np.float32)
    head_of = np.arange(P) // DK
    head_mask = (head_of[:, None] == np.arange(HH)[None, :]).astype(np.float32)
    pick = np.zeros((P, DK, P), np.float32)
    for d in range(DK):
        pick[d * HH + head_of, d, np.arange(P)] = 1.0
    return ident, head_mask, pick


def kernel(**inputs):
    import concourse.bacc as _bacc
    from concourse import mybir as _mybir
    from concourse.bass_utils import run_bass_kernel_spmd as _run

    a = {k: np.asarray(v) for k, v in inputs.items()}

    def by_value_feature(w):
        return w.reshape(HALVES, HH, DK, -1).transpose(0, 2, 1, 3).reshape(D, -1)

    w_qkv = a["L0_attn_W_qkv"]
    w_qkv = np.concatenate([w_qkv[:2 * D], by_value_feature(w_qkv[2 * D:])]).T
    w_o = by_value_feature(a["L0_attn_W_o"].T)
    w_ltm = a["L0_attn_W_LTM"].reshape(HALVES, HH, DK, DK).transpose(1, 3, 0, 2).reshape(P, HALVES * DK)
    names = ["V_gs", "V_T0", "beta_tau", "beta_gm", "C_ch", "gamma"]
    by_head = np.stack([a["L0_attn_" + n].reshape(HALVES, HH).T for n in names], 1)
    head_params = np.repeat(by_head, DK, 0)
    shared = np.broadcast_to(np.concatenate([a["L0_attn_alpha_ppd"], a["L0_attn_IC_threshold"]])[None], (P, 2))
    ident, head_mask, pick = constants()
    given = {
        "x": a["L0_attn_x"].reshape(B * L, D), "w_qkv": w_qkv, "w_o": w_o, "w_fc": a["L0_ffn_W_fc"].T,
        "w_proj": a["L0_ffn_W_proj"].T, "w_ltm": w_ltm, "head_params": head_params, "shared_params": shared,
        "ident": ident, "head_mask": head_mask, "pick": pick,
    }
    nc = _bacc.Bacc("TRN2", target_bir_lowering=False, num_devices=1)
    arrays, args = {}, []
    for name, value in given.items():
        value = np.ascontiguousarray(value)
        arrays[f"in_{name}"] = value
        args.append(nc.dram_tensor(f"in_{name}", value.shape, _mybir.dt.from_np(value.dtype),
                                   kind="ExternalInput").ap())
    out = nc.dram_tensor("out", (B * L, D), _mybir.dt.float32, kind="ExternalOutput").ap()
    build(nc, *args, out)
    r = _run(nc, [arrays], core_ids=[0])
    return r.results[0]["out"].reshape(B, L, D)
```

```python
from contextlib import ExitStack

import numpy as np

import concourse.bass as bass
from concourse import mybir

F32 = mybir.dt.float32
F32R = mybir.dt.float32r
ALU = mybir.AluOpType
ACT = mybir.ActivationFunctionType
AX = mybir.AxisListType

B, L, D, H, DK, F = 8, 512, 256, 16, 16, 1024
P = 128
KT = D // P
HALVES = KT
HH = H // HALVES
TILES = L // P
FT = F // P
GRP = 4
SLOTS = 16
HS = SLOTS // HALVES
NS = 4
NZ = 8
LN_EPS = 1e-5
STEPS, BETA, THRESHOLD = 5, 0.9, 1.0


def spike_count(y):
    mem, spikes = np.float32(0), 0
    for _ in range(STEPS):
        reset = np.float32(mem - np.float32(THRESHOLD) > 0)
        mem = np.float32(np.float32(BETA) * mem + y) - reset * np.float32(THRESHOLD)
        spikes += int(mem - np.float32(THRESHOLD) > 0)
    return spikes


def spike_drives():
    out = []
    for k in range(1, STEPS + 1):
        low, high = np.float32(0), np.float32(2)
        while np.nextafter(low, high, dtype=np.float32) < high:
            mid = np.float32((low + high) / 2)
            low, high = (mid, high) if spike_count(mid) < k else (low, mid)
        out.append(float(low))
    return out


DRIVES = spike_drives()


def step_features(s):
    j = s % HS
    first = j // 2 + 8 * (j % 2)
    return s // HS, (first, first + 4)


def build(nc, x, w_qkv, w_o, w_fc, w_proj, w_ltm, head_params, shared_params, ident, head_mask, pick, out):
    ctx = ExitStack()
    with ctx:
        def sb(name, shape, dt=F32):
            return ctx.enter_context(nc.sbuf_tensor(name, shape, dt))

        def ps(name, shape):
            return ctx.enter_context(nc.psum_tensor(name, shape, F32))

        def sem(name):
            return ctx.enter_context(nc.semaphore(name))

        wqkv_s = sb("wqkv_s", [P, 2, KT, 3 * D], F32R)
        wfc_s = sb("wfc_s", [P, 2, KT, F], F32R)
        wo_sb = sb("wo_sb", [P, HALVES, D])
        wproj_sb = sb("wproj_sb", [P, FT, D])
        pick_sb = sb("pick_sb", [P, DK, P], F32R)
        ident_sb = sb("ident_sb", [P, P])
        mask_sb = sb("mask_sb", [P, HH])
        mean_sb = sb("mean_sb", [P, HH])
        wt = sb("wt", [P, HALVES * DK])
        hp = sb("hp", [P, 6, HALVES])
        shp = sb("shp", [P, 2])
        vn = sb("vn", [P, HALVES * DK])
        absv, zt, goc, marg, signm, sp_v, t0, t1, t2 = (
            sb(name, [P, HALVES * DK]) for name in "absv zt goc marg signm sp_v t0 t1 t2".split())
        gvt = sb("gvt", [P, HALVES])
        rch = sb("rch", [P, HALVES])
        ret = sb("ret", [P, HALVES * DK])
        coef = sb("coef", [P, HALVES * DK])
        wblk = sb("wblk", [P, HALVES, DK, HH])
        summer = sb("summer", [P, HALVES, 4, GRP, 4 * HH])
        eps_sb = sb("eps_sb", [P, 2])
        ksum = sb("ksum", [P, KT, H])

        stats = [sb(f"stats{i}", [P, TILES, 6]) for i in range(4)]
        moments = [sb(f"moments{i}", [P, 3, TILES]) for i in range(4)]
        dev = [sb(f"dev{i}", [P, TILES]) for i in range(4)]
        rdev = [sb(f"rdev{i}", [P, TILES]) for i in range(4)]
        nmr = [sb(f"nmr{i}", [P, TILES]) for i in range(4)]

        xa = sb("xa", [P, TILES, D])
        xf = sb("xf", [P, KT, L])
        xt = sb("xt", [P, 2, KT, L], F32R)
        kc = sb("kc", [P, L])
        ksq = sb("ksq", [P, L])
        kdev = sb("kdev", [P, TILES * HH])
        krd = sb("krd", [P, TILES * HH])
        krx = sb("krx", [P, TILES * HH, DK])
        kf = sb("kf", [P, HALVES, L])
        qf = sb("qf", [P, HALVES, L])
        vf = sb("vf", [P, L])
        vh = sb("vh", [P, HALVES, L], F32R)
        vl = sb("vl", [P, HALVES, L], F32R)
        hebb = sb("hebb", [P, 2, 2, L])
        state = sb("state", [P, NS, 2, L])
        prod = sb("prod", [P, NZ, 2, L])
        yt = sb("yt", [P, HALVES, L])
        oo = sb("oo", [P, TILES, D])
        x1 = sb("x1", [P, TILES, D])
        x1k = sb("x1k", [P, TILES, D])
        x1f = sb("x1f", [P, KT, L])
        x1t = sb("x1t", [P, 2, KT, L], F32R)
        hr = sb("hr", [P, 2, L])
        ht = sb("ht", [P, FT, L])
        yf = sb("yf", [P, TILES, D])
        spk = sb("spk", [P, TILES, D])

        raw = prod[:, :, :, :].rearrange("p z i l -> p (z i l)")
        wfc_raw = raw[:, 0:KT * F].rearrange("p (t n) -> p t n", t=KT)
        wqkv_raw = hebb[:, :, :, :].rearrange("p z i l -> p (z i l)")[:, 0:KT * 3 * D].rearrange(
            "p (t n) -> p t n", t=KT)

        p_rep = [ps(f"p_rep{i}", [P, 2, L]) for i in range(2)]
        p_y = ps("p_y", [P, L])
        p_a = ps("p_a", [P, L])
        p_c = [ps(f"p_c{i}", [P, L]) for i in range(2)]

        S = {name: sem(name) for name in """
            x_in params_in tables_in weights_in again_in out_done keep_done
            setup_ready setup_exp centred qkv_high qkv_low wide_high wide_low tables_done setup_step
            n1_stats n1_diff n1_var n1_dev n1_step n1_done  xt_turned xt_done xt_high xt_low
            k_proj k_sq k_var k_dev k_rdev k_spread k_scale k_done  v_proj v_done  q_proj q_done
            pick_in v_high v_low
            rep_done hebb_done state_done prod_done sum_done y_done
            o_proj o_done n2_stats n2_diff n2_var n2_dev n2_step n2_done x1_done
            n3_stats n3_diff n3_var n3_dev n3_step n3_done  x1_turned x1t_done x1t_high x1t_low
            up_done relu_done h_done down_done yf_done
            spike_step n4_stats n4_diff n4_var n4_dev n4_step n4_done res_done""".split()}

        def at(value):
            return max(value, 0) if isinstance(value, int) else value

        def run(eng, iteration):
            iteration(0, True, False, False, True)
            iteration(1, True, True, False, True)
            iteration(2, True, True, True, True)
            with eng.Fori(3, B - 1) as g:
                iteration(g, True, True, True, True)
            iteration(B - 1, True, True, True, False)
            iteration(B, False, True, True, False)
            iteration(B + 1, False, False, True, False)

        def tokens(u):
            return slice(u * P, (u + 1) * P)

        def by_tile(a, b):
            return a[bass.ds(b * L, L), :].rearrange("(u p) d -> p u d", p=P)

        PASSES = ((0, 0), (0, 1), (1, 0))

        block = ctx.enter_context(nc.Block())

        @block.sync
        def _(sp):
            sp.dma_start(xa[:, :, :], by_tile(x, 0)).then_inc(S["x_in"], 16)
            sp.dma_start(ident_sb[:, :], ident).then_inc(S["tables_in"], 16)
            sp.dma_start(wqkv_raw, w_qkv.rearrange("(t p) n -> p t n", p=P)).then_inc(S["tables_in"], 16)
            sp.dma_start(mask_sb[:, :], head_mask).then_inc(S["tables_in"], 16)
            sp.dma_start(wt[:, :], w_ltm).then_inc(S["params_in"], 16)
            sp.dma_start(hp[:, :, :], head_params).then_inc(S["params_in"], 16)
            sp.dma_start(shp[:, :], shared_params).then_inc(S["params_in"], 16)
            sp.dma_start(wo_sb[:, :, :], w_o.rearrange("(t p) n -> p t n", p=P)).then_inc(S["weights_in"], 16)
            sp.dma_start(wfc_raw, w_fc.rearrange("(t p) n -> p t n", p=P)).then_inc(S["weights_in"], 16)
            sp.dma_start(wproj_sb[:, :, :], w_proj.rearrange("(t p) n -> p t n", p=P)).then_inc(S["weights_in"], 16)

            def load_x(b):
                sp.wait_ge(S["xt_turned"], at(KT * b))
                sp.dma_start(xa[:, :, :], by_tile(x, b)).then_inc(S["x_in"], 16)

            def iteration(g, now, before, two_before, after):
                if two_before:
                    sp.wait_ge(S["res_done"], at(g - 1))
                    sp.dma_start(by_tile(out, g - 2), x1k[:, :, :]).then_inc(S["out_done"], 16)
                if before:
                    if not two_before: sp.wait_ge(S["x1_done"], at(g))
                    sp.wait_ge(S["out_done"], at(16 * (g - 1)))
                    sp.dma_start(x1k[:, :, :], x1[:, :, :]).then_inc(S["keep_done"], 16)
                if now:
                    if not two_before: sp.wait_ge(S["n3_done"], at(TILES * g))
                    sp.wait_ge(S["keep_done"], at(16 * g))
                    sp.dma_start(x1[:, :, :], by_tile(x, g)).then_inc(S["again_in"], 16)

            load_x(1)
            for g in range(3):
                load_x(g + 2)
                iteration(g, True, g > 0, g > 1, True)
            with sp.Fori(3, B - 2) as g:
                load_x(g + 2)
                iteration(g, True, True, True, True)
            for g in range(B - 2, B + 2):
                iteration(g, g < B, g < B + 1, True, g < B - 1)
            sp.wait_ge(S["out_done"], at(16 * B))

        @block.tensor
        def _(pe):
            def turn_x(b, t):
                pe.wait_ge(S["k_done"], at(2 * b))
                pe.wait_ge(S["xt_done"], at(KT * b + t))
                pe.wait_ge(S["n1_done"], at(TILES * (b + 1)))
                for u in range(TILES):
                    last = pe.transpose(p_a[:, tokens(u)], xa[:, u, t * P:(t + 1) * P], ident_sb[:, :])
                last.then_inc(S["xt_turned"], 1)

            def project(b, first_col, done):
                for t in range(KT):
                    for i, j in PASSES:
                        last = pe.matmul(p_a[:, :], wqkv_s[:, i, t, first_col:first_col + P], xt[:, j, t, :],
                                         start=(t == i == j == 0), stop=(t == KT - 1 and i == 1))
                last.then_inc(S[done], 1)

            def project_k(b, half):
                pe.wait_ge(S["xt_low"], at(KT * (b + 1)))
                pe.wait_ge(S["k_done"], at(2 * b + half))
                project(b, D + half * P, "k_proj")

            def project_v(b, half):
                pe.wait_ge(S["k_dev"], at(2 * b + half + 1))
                project(b, 2 * D + half * P, "v_proj")

            def project_q(b, half):
                pe.wait_ge(S["v_done"], at(2 * b + half + 1))
                project(b, half * P, "q_proj")

            def key_variance(b, half):
                pe.wait_ge(S["k_sq"], at(2 * b + half + 1))
                for u in range(TILES):
                    last = pe.matmul(p_a[:, u * HH:(u + 1) * HH], ksq[:, u * P:(u + 1) * P], mean_sb[:, :],
                                     start=True, stop=True)
                last.then_inc(S["k_var"], 1)

            def key_scale(b, half):
                pe.wait_ge(S["k_spread"], at(2 * b + half + 1))
                pe.wait_ge(S["q_done"], at(2 * b + half + 1))
                for u in range(TILES):
                    scale = krx[:, u * HH:(u + 1) * HH, :].rearrange("p h e -> p (h e)")
                    last = pe.transpose(p_a[:, tokens(u)], scale, ident_sb[:, :])
                last.then_inc(S["k_scale"], 1)

            def replicate(b, s):
                half, features = step_features(s)
                pe.wait_ge(S["hebb_done"], at(SLOTS * b + s - 1))
                if s % HS == 0:
                    pe.wait_ge(S["v_low"], at(2 * b + half + 1))
                for i, d in enumerate(features):
                    pe.matmul(p_rep[s % 2][:, i, :], pick_sb[:, d, :], vh[:, half, :], start=True, stop=False)
                    last = pe.matmul(p_rep[s % 2][:, i, :], pick_sb[:, d, :], vl[:, half, :], start=False, stop=True)
                last.then_inc(S["rep_done"], 1)

            def sums(b, m):
                half, dl = m // 4, m % 4
                if dl == 0:
                    pe.wait_ge(S["y_done"], at(2 * b + half))
                    pe.wait_ge(S["q_done"], at(2 * b + half + 1))
                    pe.matmul(p_y[:, :], wblk[:, half, :, :].rearrange("p d h -> p (d h)"), qf[:, half, :],
                              start=True, stop=False, skip_group_check=True)
                pe.wait_ge(S["prod_done"], at(SLOTS * b + 2 * m + 2))
                for grp in range(GRP):
                    s = 2 * m + grp // 2
                    last = pe.matmul(p_y[32 * grp:32 * grp + 32, :], summer[:, half, dl, grp, :],
                                     prod[:, s % NZ, grp % 2, :], start=False, stop=(dl == 3),
                                     skip_group_check=True)
                last.then_inc(S["sum_done"], 1)

            def project_out(b, t):
                pe.wait_ge(S["relu_done"], at(FT * b - 1 + t))
                pe.wait_ge(S["y_done"], at(2 * (b + 1)))
                for i in range(2):
                    for half in range(HALVES):
                        last = pe.matmul(p_c[(t + 1) % 2][:, i * D:(i + 1) * D], yt[:, half, tokens(2 * t + i)],
                                         wo_sb[:, half, :], start=(half == 0), stop=(half == HALVES - 1))
                last.then_inc(S["o_proj"], 1)

            def down(b, u, part, next_too):
                if part == 0:
                    if u < 2:
                        if u == 0: pe.wait_ge(S["h_done"], at(FT * (b + 1)))
                        if next_too: pe.wait_ge(S["o_done"], at(2 * (b + 1) + u + 1))
                    else:
                        pe.wait_ge(S["yf_done"], at(TILES * b + u - 1))
                for f in range(part * FT // 2, (part + 1) * FT // 2):
                    last = pe.matmul(p_c[(u + 1) % 2][:, 0:D], ht[:, f, tokens(u)], wproj_sb[:, f, :],
                                     start=(f == 0), stop=(f == FT - 1))
                if part == 1:
                    last.then_inc(S["down_done"], 1)

            def turn_x1(b, t):
                pe.wait_ge(S["n3_done"], at(TILES * (b + 1)))
                pe.wait_ge(S["o_done"], at(2 * (b + 1)))
                pe.wait_ge(S["yf_done"], at(TILES * (b - 1) + 3 + t))
                for u in range(TILES):
                    last = pe.transpose(p_c[(t + 1) % 2][:, tokens(u)], oo[:, u, t * P:(t + 1) * P], ident_sb[:, :])
                last.then_inc(S["x1_turned"], 1)

            def up(b, f):
                pe.wait_ge(S["x1t_low"], at(KT * (b + 1)))
                pe.wait_ge(S["relu_done"], at(FT * b + f - 1))
                for t in range(KT):
                    for i, j in PASSES:
                        last = pe.matmul(p_c[(f + 1) % 2][:, :], wfc_s[:, i, t, f * P:(f + 1) * P], x1t[:, j, t, :],
                                         start=(t == i == j == 0), stop=(t == KT - 1 and i == 1))
                last.then_inc(S["up_done"], 1)

            pe.wait_ge(S["tables_in"], 48)
            turn_x(0, 0)
            turn_x(0, 1)
            pe.wait_ge(S["qkv_low"], 1)
            project_k(0, 0)
            key_variance(0, 0)
            project_v(0, 0)
            project_q(0, 0)
            key_scale(0, 0)
            pe.wait_ge(S["weights_in"], 48)
            pe.wait_ge(S["pick_in"], 16)
            replicate(0, 0)
            pe.wait_ge(S["tables_done"], 1)
            pe.wait_ge(S["wide_low"], 1)

            def iteration(g, now, before, two_before, after):
                b, b1, b2 = g + 1, g - 1, g - 2
                for s in range(SLOTS):
                    if now and s < SLOTS - 1: replicate(g, s + 1)
                    if before and s in (0, 2): sums(b1, 6 + s // 2)
                    if now and s >= 4 and s % 2 == 0: sums(g, (s - 4) // 2)
                    if two_before and s == 1: up(b2, 4)
                    if now:
                        if s == 0: project_k(g, 1)
                        if s == 1: key_variance(g, 1)
                        if s == 2: project_v(g, 1)
                        if s == 3: project_q(g, 1)
                    if two_before:
                        if s == 0: up(b2, 3)
                        if s == 1: up(b2, 5)
                        if s in (2, 3): up(b2, 4 + s)
                    if before and s in (4, 5): project_out(b1, s - 4)
                    if now and s == 5: key_scale(g, 1)
                    if two_before:
                        if s in (5, 6): down(b2, 0, s - 5, before)
                        if s in (6, 7): down(b2, 1, s - 6, before)
                        if 8 <= s < 12: down(b2, s // 2 - 2, s % 2, before)
                    if before and s == 12:
                        turn_x1(b1, 0)
                        turn_x1(b1, 1)
                    if after:
                        if s in (7, 8): turn_x(b, s - 7)
                        if s == 10: project_k(b, 0)
                        if s == 11: key_variance(b, 0)
                        if s == 12: project_v(b, 0)
                        if s == 13: project_q(b, 0)
                        if s == 14: key_scale(b, 0)
                    if before:
                        if s == 14: up(b1, 0)
                        if s == 15:
                            up(b1, 1)
                            up(b1, 2)
                    if after and s == SLOTS - 1: replicate(b, 0)

            run(pe, iteration)

        @block.scalar
        def _(act):
            act.wait_ge(S["setup_ready"], 1)
            nc.scalar.activation(zt[:, :], absv[:, :], ACT.Exp, scale=-1.0).then_inc(S["setup_exp"], 1)
            act.wait_ge(S["setup_ready"], 2)
            nc.scalar.activation(ret[:, :], goc[:, :], ACT.Exp, scale=-1.0)
            nc.scalar.activation(signm[:, :], marg[:, :], ACT.Tanh).then_inc(S["setup_exp"], 1)

            def deviation(n, b):
                act.wait_ge(S[f"n{n}_var"], at(b + 1))
                eps = eps_sb[:, 1:2] if n == 4 else eps_sb[:, 0:1]
                nc.scalar.activation(dev[n - 1][:, :], moments[n - 1][:, 2, :], ACT.Sqrt, bias=eps,
                                     scale=1.0 / D).then_inc(S[f"n{n}_dev"], 1)

            def norm(n, b, src, dst, used, count):
                act.wait_ge(S[f"n{n}_step"], at(2 * (b + 1)))
                act.wait_ge(S[used], at(count))
                for u in range(TILES):
                    nc.scalar.activation(dst[:, u, :], src[:, u, :], ACT.Identity, scale=rdev[n - 1][:, u:u + 1],
                                         bias=nmr[n - 1][:, u:u + 1]).then_inc(S[f"n{n}_done"], 1)

            def copy(src, dst, ready, count, done):
                act.wait_ge(S[ready], at(count))
                nc.scalar.copy(dst, src).then_inc(S[done], 1)

            def norm1(b):
                norm(1, b, xa, xa, "x_in", 16 * (b + 1))

            def copy_xt(b, t):
                act.wait_ge(S["xt_low"], at(KT * (b - 1) + t + 1))
                copy(p_a[:, :], xf[:, t, :], "xt_turned", KT * b + t + 1, "xt_done")
                copy(xf[:, t, :], xt[:, 0, t, :], "xt_done", KT * b + t + 1, "xt_high")

            def square_k(b, half):
                act.wait_ge(S["k_proj"], at(2 * b + half + 1))
                act.wait_ge(S["k_done"], at(2 * b + half))
                nc.scalar.copy(kc[:, :], p_a[:, :])
                nc.scalar.activation(ksq[:, :], p_a[:, :], ACT.Square).then_inc(S["k_sq"], 1)

            def key_deviation(b, half):
                act.wait_ge(S["k_var"], at(2 * b + half + 1))
                nc.scalar.activation(kdev[:, :], p_a[:, 0:TILES * HH], ACT.Sqrt, bias=eps_sb[:, 0:1]).then_inc(
                    S["k_dev"], 1)

            def copy_v(b, half):
                act.wait_ge(S["v_low"], at(2 * b + half))
                copy(p_a[:, :], vf[:, :], "v_proj", 2 * b + half + 1, "v_done")
                copy(vf[:, :], vh[:, half, :], "v_done", 2 * b + half + 1, "v_high")

            def copy_q(b, half):
                act.wait_ge(S["prod_done"], at(SLOTS * (b - 1) + HS * (half + 1)))
                copy(p_a[:, :], qf[:, half, :], "q_proj", 2 * b + half + 1, "q_done")

            def copy_y(b, half):
                act.wait_ge(S["o_proj"], at(2 * b))
                copy(p_y[:, :], yt[:, half, :], "sum_done", HS * b + 4 * (half + 1), "y_done")

            def copy_o(b, t):
                act.wait_ge(S["x1_turned"], at(KT * b))
                copy(p_c[(t + 1) % 2][:, :], oo[:, 2 * t:2 * t + 2, :].rearrange("p u d -> p (u d)"), "o_proj",
                     2 * b + t + 1, "o_done")

            def copy_x1t(b, t):
                act.wait_ge(S["x1t_low"], at(KT * (b - 1) + t + 1))
                copy(p_c[(t + 1) % 2][:, :], x1f[:, t, :], "x1_turned", KT * b + t + 1, "x1t_done")
                copy(x1f[:, t, :], x1t[:, 0, t, :], "x1t_done", KT * b + t + 1, "x1t_high")

            def hidden(b, f):
                act.wait_ge(S["up_done"], at(FT * b + f + 1))
                act.wait_ge(S["h_done"], at(FT * b + f - 1))
                nc.scalar.activation(hr[:, f % 2, :], p_c[(f + 1) % 2][:, :], ACT.Relu).then_inc(S["relu_done"], 1)
                act.wait_ge(S["relu_done"], at(FT * b + f + 1))
                nc.scalar.activation(ht[:, f, :], hr[:, f % 2, :], ACT.Square).then_inc(S["h_done"], 1)

            def copy_yf(b, u):
                act.wait_ge(S["n4_step"], at(2 * b))
                copy(p_c[(u + 1) % 2][:, 0:D], yf[:, u, :], "down_done", TILES * b + u + 1, "yf_done")

            deviation(1, 0)
            norm1(0)
            act.wait_ge(S["centred"], KT)
            nc.scalar.copy(wqkv_s[:, 0, :, :], wqkv_raw).then_inc(S["qkv_high"], 1)
            copy_xt(0, 0)
            copy_xt(0, 1)
            square_k(0, 0)
            key_deviation(0, 0)
            copy_v(0, 0)
            copy_q(0, 0)
            act.wait_ge(S["weights_in"], 48)
            nc.scalar.copy(wfc_s[:, 0, :, :], wfc_raw).then_inc(S["wide_high"], 1)

            def iteration(g, now, before, two_before, after):
                b, b1, b2 = g + 1, g - 1, g - 2
                for s in range(SLOTS):
                    if now and s == 0: square_k(g, 1)
                    if two_before and s == 0: hidden(b2, 3)
                    if two_before and s == 1: hidden(b2, 4)
                    if now and s == 1: key_deviation(g, 1)
                    if two_before and s == 1: hidden(b2, 5)
                    if now and s == 2: copy_v(g, 1)
                    if before and s == 3: copy_y(b1, 1)
                    if now and s == 3: copy_q(g, 1)
                    if two_before and s in (2, 3): hidden(b2, 4 + s)
                    if after and s == 3: deviation(1, b)
                    if before and s in (4, 5): copy_o(b1, s - 4)
                    if after and s == 5: norm1(b)
                    if before and s == 6: deviation(2, b1)
                    if two_before and s == 6: copy_yf(b2, 0)
                    if before and s == 7: norm(2, b1, oo, oo, "x1_done", b1)
                    if two_before and s in (7, 9, 11): copy_yf(b2, (s - 5) // 2)
                    if after and s in (7, 8): copy_xt(b, s - 7)
                    if before and s == 10: deviation(3, b1)
                    if after and s == 10: square_k(b, 0)
                    if now and s == 11: copy_y(g, 0)
                    if after and s == 11: key_deviation(b, 0)
                    if before and s == 11: norm(3, b1, x1, oo, "x1_done", b1 + 1)
                    if before and s == 12:
                        copy_x1t(b1, 0)
                        copy_x1t(b1, 1)
                    if after and s == 12: copy_v(b, 0)
                    if after and s == 13: copy_q(b, 0)
                    if before and s == 14: hidden(b1, 0)
                    if before and s == 15:
                        hidden(b1, 1)
                        hidden(b1, 2)
                    if two_before and s == 15:
                        deviation(4, b2)
                        norm(4, b2, spk, spk, "res_done", b2)

            run(act, iteration)

        @block.vector
        def _(dve):
            v = nc.vector
            steps = [0]

            def step(ins):
                steps[0] += 1
                ins.then_inc(S["setup_step"], 1)
                dve.wait_ge(S["setup_step"], steps[0])

            def statistics(n, b, src, ready, count):
                dve.wait_ge(S[ready], at(count))
                dve.wait_ge(S[f"n{n}_var"], at(b))
                for u in range(TILES):
                    last = v.bn_stats(stats[n - 1][:, u, :], src[:, u, :])
                last.then_inc(S[f"n{n}_stats"], 1)
                dve.wait_ge(S[f"n{n}_stats"], at(b + 1))
                dve.wait_ge(S[f"n{n}_step"], at(2 * b))
                st, mo = stats[n - 1], moments[n - 1]
                v.tensor_tensor(mo[:, 0, :], st[:, :, 1], st[:, :, 4], ALU.add)
                v.tensor_tensor(mo[:, 1, :], st[:, :, 1], st[:, :, 4], ALU.subtract).then_inc(S[f"n{n}_diff"], 1)
                v.tensor_tensor(mo[:, 2, :], st[:, :, 2], st[:, :, 5], ALU.add).then_inc(S[f"n{n}_diff"], 1)
                dve.wait_ge(S[f"n{n}_diff"], at(3 * b + 1))
                v.scalar_tensor_tensor(mo[:, 1, :], mo[:, 1, :], D / 4, mo[:, 1, :], ALU.mult, ALU.mult).then_inc(
                    S[f"n{n}_diff"], 1)
                dve.wait_ge(S[f"n{n}_diff"], at(3 * (b + 1)))
                v.tensor_tensor(mo[:, 2, :], mo[:, 2, :], mo[:, 1, :], ALU.add).then_inc(S[f"n{n}_var"], 1)

            def scales(n, b):
                dve.wait_ge(S[f"n{n}_dev"], at(b + 1))
                dve.wait_ge(S[f"n{n}_done"], at(TILES * b))
                v.reciprocal(rdev[n - 1][:, :], dev[n - 1][:, :]).then_inc(S[f"n{n}_step"], 1)
                dve.wait_ge(S[f"n{n}_step"], at(2 * b + 1))
                v.scalar_tensor_tensor(nmr[n - 1][:, :], moments[n - 1][:, 0, :], -0.5, rdev[n - 1][:, :], ALU.mult,
                                       ALU.mult).then_inc(S[f"n{n}_step"], 1)

            def key_reciprocal(b, half):
                dve.wait_ge(S["k_dev"], at(2 * b + half + 1))
                v.reciprocal(krd[:, :], kdev[:, :]).then_inc(S["k_rdev"], 1)
                dve.wait_ge(S["k_rdev"], at(2 * b + half + 1))
                v.tensor_copy(krx[:, :, :], krd[:, :].unsqueeze(2).broadcast_to([P, TILES * HH, DK])).then_inc(
                    S["k_spread"], 1)

            def norm_k(b, half):
                dve.wait_ge(S["k_scale"], at(2 * b + half + 1))
                dve.wait_ge(S["hebb_done"], at(SLOTS * (b - 1) + HS * (half + 1)))
                v.tensor_tensor(kf[:, half, :], p_a[:, :], kc[:, :], ALU.mult).then_inc(S["k_done"], 1)

            def hebbian(b, s):
                dve.wait_ge(S["rep_done"], at(SLOTS * b + s + 1))
                dve.wait_ge(S["state_done"], at(2 * (SLOTS * b + s - 1)))
                if s % HS == 0:
                    dve.wait_ge(S["k_done"], at(2 * b + s // HS + 1))
                key = kf[:, s // HS, :].unsqueeze(1).broadcast_to([P, 2, L])
                v.tensor_tensor(hebb[:, s % 2, :, :], p_rep[s % 2][:, :, :], key, ALU.mult).then_inc(
                    S["hebb_done"], 1)

            def states(b, s):
                half, features = step_features(s)
                dve.wait_ge(S["hebb_done"], at(SLOTS * b + s + 1))
                dve.wait_ge(S["prod_done"], at(SLOTS * b + s + 1 - NS))
                for i, d in enumerate(features):
                    r = half * DK + d
                    v.tensor_tensor_scan(state[:, s % NS, i, :], ret[:, r:r + 1].broadcast_to([P, L]),
                                         hebb[:, s % 2, i, :], 0.0, ALU.mult, ALU.add).then_inc(S["state_done"], 1)

            def spikes(b, pair, j):
                two = slice(2 * pair, 2 * pair + 2)
                if j == 0:
                    dve.wait_ge(S["yf_done"], at(TILES * b + 2 * (pair + 1)))
                    dve.wait_ge(S["res_done"], at(b))
                    v.tensor_scalar(spk[:, two, :], yf[:, two, :], DRIVES[0], None, ALU.is_gt).then_inc(
                        S["spike_step"], 1)
                else:
                    dve.wait_ge(S["spike_step"], at(2 * STEPS * b + STEPS * pair + j))
                    v.scalar_tensor_tensor(spk[:, two, :], yf[:, two, :], DRIVES[j], spk[:, two, :], ALU.is_gt,
                                           ALU.add).then_inc(S["spike_step"], 1)

            v.memset(eps_sb[:, 0:1], LN_EPS)
            v.memset(eps_sb[:, 1:2], LN_EPS * STEPS ** 2)
            step(v.memset(summer[:, :, :, :, :], 0.0))
            statistics(1, 0, xa, "x_in", 16)
            dve.wait_ge(S["params_in"], 48)
            step(v.tensor_tensor(gvt[:, :], hp[:, 0, :], hp[:, 1, :], ALU.subtract))
            for half in range(HALVES):
                hs = slice(half * DK, (half + 1) * DK)
                last = v.tensor_scalar(vn[:, hs], wt[:, hs], gvt[:, half:half + 1], None, ALU.add)
            step(last)
            step(v.tensor_scalar(absv[:, :], vn[:, :], -1.0, None, ALU.mult))
            v.tensor_tensor(absv[:, :], absv[:, :], vn[:, :], ALU.max).then_inc(S["setup_ready"], 1)

            dve.wait_ge(S["setup_exp"], 1)
            step(v.tensor_scalar(t0[:, :], zt[:, :], 2.0, None, ALU.add))
            step(v.reciprocal(t0[:, :], t0[:, :]))
            step(v.tensor_tensor(t0[:, :], t0[:, :], zt[:, :], ALU.mult))
            step(v.tensor_tensor(t1[:, :], t0[:, :], t0[:, :], ALU.mult))
            step(v.tensor_scalar(t2[:, :], t1[:, :], 1.0 / 15, None, ALU.mult))
            for n in (13, 11, 9, 7, 5, 3):
                step(v.scalar_tensor_tensor(t2[:, :], t2[:, :], 1.0 / n, t1[:, :], ALU.add, ALU.mult))
            step(v.scalar_tensor_tensor(t2[:, :], t2[:, :], 1.0, t0[:, :], ALU.add, ALU.mult))
            step(v.tensor_scalar(t2[:, :], t2[:, :], 2.0, None, ALU.mult))
            step(v.scalar_tensor_tensor(sp_v[:, :], vn[:, :], 0.0, t2[:, :], ALU.max, ALU.add))
            step(v.reciprocal(rch[:, :], hp[:, 4, :]))
            for half in range(HALVES):
                hs = slice(half * DK, (half + 1) * DK)
                step(v.tensor_scalar(t0[:, hs], sp_v[:, hs], hp[:, 2, half:half + 1], None, ALU.mult))
                v.tensor_scalar(goc[:, hs], t0[:, hs], rch[:, half:half + 1], None, ALU.mult)
                last = v.tensor_scalar(marg[:, hs], t0[:, hs], shp[:, 1:2], shp[:, 0:1], ALU.subtract, ALU.mult)
            last.then_inc(S["setup_ready"], 1)
            scales(1, 0)

            dve.wait_ge(S["tables_in"], 48)
            kw = wqkv_raw[:, :, D:2 * D].rearrange("p t (h e) -> p t h e", e=DK)
            v.tensor_scalar(mean_sb[:, :], mask_sb[:, :], 1.0 / DK, None, ALU.mult)
            for t in range(KT):
                last = v.tensor_reduce(ksum[:, t, :], kw[:, t, :, :], AX.X, ALU.add)
            step(last)
            step(v.tensor_scalar(ksum[:, :, :], ksum[:, :, :], 1.0 / DK, None, ALU.mult))
            for t in range(KT):
                v.tensor_tensor(kw[:, t, :, :], kw[:, t, :, :], ksum[:, t, :].unsqueeze(2).broadcast_to([P, H, DK]),
                                ALU.subtract).then_inc(S["centred"], 1)

            dve.wait_ge(S["qkv_high"], 1)
            v.tensor_tensor(wqkv_s[:, 1, :, :], wqkv_raw, wqkv_s[:, 0, :, :].bitcast(F32), ALU.subtract).then_inc(
                S["qkv_low"], 1)
            step(v.tensor_scalar(t1[:, :], zt[:, :], 1.0, None, ALU.add))
            step(v.reciprocal(t1[:, :], t1[:, :]))
            step(v.scalar_tensor_tensor(t2[:, :], vn[:, :], 0.0, zt[:, :], ALU.is_ge, ALU.max))
            step(v.tensor_tensor(t1[:, :], t1[:, :], t2[:, :], ALU.mult))
            for half in range(HALVES):
                hs = slice(half * DK, (half + 1) * DK)
                step(v.scalar_tensor_tensor(t0[:, hs], sp_v[:, hs], hp[:, 3, half:half + 1], t1[:, hs], ALU.mult,
                                            ALU.mult))
            dve.wait_ge(S["setup_exp"], 2)
            for half in range(HALVES):
                hs = slice(half * DK, (half + 1) * DK)
                step(v.scalar_tensor_tensor(coef[:, hs], signm[:, hs], hp[:, 5, half:half + 1], t0[:, hs], ALU.mult,
                                            ALU.mult))
            key_reciprocal(0, 0)
            norm_k(0, 0)
            mask = mask_sb[:, :].unsqueeze(1)
            for half in range(HALVES):
                hs = slice(half * DK, (half + 1) * DK)
                v.tensor_tensor(wblk[:, half, :, :], mask.broadcast_to([P, DK, HH]),
                                wt[:, hs].unsqueeze(2).broadcast_to([P, DK, HH]), ALU.mult)
                for dl in range(4):
                    by_group = coef[:, hs].rearrange("p (g l) -> p g l", g=GRP)[:, :, dl]
                    last = v.tensor_tensor(summer[:, half, dl, :, dl * HH:(dl + 1) * HH],
                                           mask.broadcast_to([P, GRP, HH]),
                                           by_group.unsqueeze(2).broadcast_to([P, GRP, HH]), ALU.mult)
            last.then_inc(S["tables_done"], 1)
            dve.wait_ge(S["tables_done"], 1)

            def iteration(g, now, before, two_before, after):
                b, b1, b2 = g + 1, g - 1, g - 2
                for s in range(SLOTS):
                    ends = (g, s - 1) if s > 0 else (b1, SLOTS - 1)
                    if now: hebbian(g, s)
                    if now if s > 0 else before: states(*ends)
                    if after and s == 2: statistics(1, b, xa, "x_in", 16 * (b + 1))
                    if now and s == 3: key_reciprocal(g, 1)
                    if after and s == 4: scales(1, b)
                    if before and s == 6: statistics(2, b1, oo, "o_done", 2 * (b1 + 1))
                    if now and s == 6: norm_k(g, 1)
                    if before and s == 7: scales(2, b1)
                    if two_before and s in (9, 13):
                        for j in (0, 1, 2): spikes(b2, s // 12, j)
                    if before and s == 10: statistics(3, b1, x1, "x1_done", b1 + 1)
                    if before and s == 11: scales(3, b1)
                    if two_before and s in (11, 14):
                        for j in (3, 4): spikes(b2, s // 12, j)
                    if after and s == 13: key_reciprocal(b, 0)
                    if two_before and s == 15: statistics(4, b2, spk, "spike_step", 2 * STEPS * (b2 + 1))
                    if after and s == 15: norm_k(b, 0)
                    if two_before and s == 15: scales(4, b2)

            run(dve, iteration)

        @block.gpsimd
        def _(pool):
            p = nc.gpsimd

            def read(b, s):
                pool.wait_ge(S["state_done"], at(2 * (SLOTS * b + s + 1)))
                pool.wait_ge(S["sum_done"], at(HS * b + s // 2 - 1))
                if s % HS == 0:
                    pool.wait_ge(S["q_done"], at(2 * b + s // HS + 1))
                p.tensor_tensor(prod[:, s % NZ, :, :], state[:, s % NS, :, :],
                                qf[:, s // HS, :].unsqueeze(1).broadcast_to([P, 2, L]), ALU.mult).then_inc(
                    S["prod_done"], 1)

            def add_attention(b):
                pool.wait_ge(S["n2_done"], at(TILES * (b + 1)))
                pool.wait_ge(S["again_in"], at(16 * (b + 1)))
                p.tensor_tensor(x1[:, :, :], x1[:, :, :], oo[:, :, :], ALU.add).then_inc(S["x1_done"], 1)

            def add_feed_forward(b):
                pool.wait_ge(S["n4_done"], at(TILES * (b + 1)))
                pool.wait_ge(S["keep_done"], at(16 * (b + 1)))
                p.tensor_tensor(x1k[:, :, :], x1k[:, :, :], spk[:, :, :], ALU.add).then_inc(S["res_done"], 1)

            def rest(value, high, low, ready, count, done):
                pool.wait_ge(S[ready], at(count))
                p.tensor_tensor(low, value, high.bitcast(F32), ALU.subtract).then_inc(S[done], 1)

            def low_x(b, t):
                rest(xf[:, t, :], xt[:, 0, t, :], xt[:, 1, t, :], "xt_high", KT * b + t + 1, "xt_low")

            def low_x1(b, t):
                rest(x1f[:, t, :], x1t[:, 0, t, :], x1t[:, 1, t, :], "x1t_high", KT * b + t + 1, "x1t_low")

            def low_v(b, half):
                rest(vf[:, :], vh[:, half, :], vl[:, half, :], "v_high", 2 * b + half + 1, "v_low")

            p.dma_start(pick_sb[:, :, :], pick).then_inc(S["pick_in"], 16)
            low_x(0, 0)
            low_x(0, 1)
            low_v(0, 0)
            rest(wfc_raw, wfc_s[:, 0, :, :], wfc_s[:, 1, :, :], "wide_high", 1, "wide_low")
            pool.wait_ge(S["wide_low"], 1)

            def iteration(g, now, before, two_before, after):
                b, b1, b2 = g + 1, g - 1, g - 2
                for s in range(SLOTS):
                    if s > 0 and now: read(g, s - 1)
                    if s == 0 and before: read(b1, SLOTS - 1)
                    if now and s == 4: low_v(g, 1)
                    if before and s == 8: add_attention(b1)
                    if after and s in (8, 9): low_x(b, s - 8)
                    if before and s == 13:
                        low_x1(b1, 0)
                        low_x1(b1, 1)
                    if after and s == 14: low_v(b, 0)
                    if two_before and s == 15: add_feed_forward(b2)

            run(pool, iteration)


def constants():
    ident = np.eye(P, dtype=np.float32)
    head_of = np.arange(P) // DK
    head_mask = (head_of[:, None] == np.arange(HH)[None, :]).astype(np.float32)
    pick = np.zeros((P, DK, P), np.float32)
    for d in range(DK):
        pick[d * HH + head_of, d, np.arange(P)] = 1.0
    return ident, head_mask, pick


def kernel(**inputs):
    import concourse.bacc as _bacc
    from concourse import mybir as _mybir
    from concourse.bass_utils import run_bass_kernel_spmd as _run

    a = {k: np.asarray(v) for k, v in inputs.items()}

    def by_value_feature(w):
        return w.reshape(HALVES, HH, DK, -1).transpose(0, 2, 1, 3).reshape(D, -1)

    w_qkv = a["L0_attn_W_qkv"]
    w_qkv = np.concatenate([w_qkv[:2 * D], by_value_feature(w_qkv[2 * D:])]).T
    w_o = by_value_feature(a["L0_attn_W_o"].T)
    w_ltm = a["L0_attn_W_LTM"].reshape(HALVES, HH, DK, DK).transpose(1, 3, 0, 2).reshape(P, HALVES * DK)
    names = ["V_gs", "V_T0", "beta_tau", "beta_gm", "C_ch", "gamma"]
    by_head = np.stack([a["L0_attn_" + n].reshape(HALVES, HH).T for n in names], 1)
    head_params = np.repeat(by_head, DK, 0)
    shared = np.broadcast_to(np.concatenate([a["L0_attn_alpha_ppd"], a["L0_attn_IC_threshold"]])[None], (P, 2))
    ident, head_mask, pick = constants()
    given = {
        "x": a["L0_attn_x"].reshape(B * L, D), "w_qkv": w_qkv, "w_o": w_o, "w_fc": a["L0_ffn_W_fc"].T,
        "w_proj": a["L0_ffn_W_proj"].T, "w_ltm": w_ltm, "head_params": head_params, "shared_params": shared,
        "ident": ident, "head_mask": head_mask, "pick": pick,
    }
    nc = _bacc.Bacc("TRN2", target_bir_lowering=False, num_devices=1)
    arrays, args = {}, []
    for name, value in given.items():
        value = np.ascontiguousarray(value)
        arrays[f"in_{name}"] = value
        args.append(nc.dram_tensor(f"in_{name}", value.shape, _mybir.dt.from_np(value.dtype),
                                   kind="ExternalInput").ap())
    out = nc.dram_tensor("out", (B * L, D), _mybir.dt.float32, kind="ExternalOutput").ap()
    build(nc, *args, out)
    r = _run(nc, [arrays], core_ids=[0])
    return r.results[0]["out"].reshape(B, L, D)
```
